# Optimizing a Trainium2 kernel written in Bass

```python
import numpy as np
import jax
import jax.numpy as jnp

def _softmax(x, axis=-1):
    return jax.nn.softmax(x, axis=axis)

def _gelu(x):
    return jax.nn.gelu(x, approximate=True)

def _silu(x):
    return jax.nn.silu(x)

def _sigmoid(x):
    return jax.nn.sigmoid(x)

def _layernorm(x, axis=-1, eps=1e-05):
    m = jnp.mean(x, axis=axis, keepdims=True)
    v = jnp.var(x, axis=axis, keepdims=True)
    return (x - m) / jnp.sqrt(v + eps)

def _scatter_add(tgt, idx, src, axis=0):
    return tgt.at[idx].add(src)

def _segment_sum(src, seg, n):
    return jax.ops.segment_sum(src, seg, n)
kernel_name = 'mk_adj_resnorm_d2_adj_r2_bc81e4'

def setup_inputs(seed: int=0):
    np.random.seed(seed)
    _w = jnp.asarray

    def _rec_inputs():
        import jax
        import jax.numpy as jnp
        _gk = jax.random.key(seed)
        x = -0.0005207 + 1.001 * jax.random.normal(jax.random.fold_in(_gk, 1), (8192, 128), jnp.float32)
        _a = jax.random.bernoulli(jax.random.fold_in(_gk, 2), 0.00195312, (8192, 8192))
        _a = jnp.logical_or(_a, jnp.swapaxes(_a, -1, -2))
        _a = jnp.logical_or(_a, jnp.eye(8192, dtype=bool))
        adj = _a.astype(jnp.int32)
        return (x, adj)
    x, adj = _rec_inputs()

    def _L0_gnn_setup():
        import jax, jax.numpy as jnp
        import numpy as np
        N = 4096
        D_IN = 128
        D_OUT = 128
        NEG_INF = -9000000000000000.0
        key = jax.random.key(seed)
        k1, k2, k3, k4 = jax.random.split(key, 4)
        node_features = jax.random.normal(k1, (N, D_IN), dtype=jnp.float32)
        adjacency_matrix = jax.random.randint(k2, (N, N), 0, 2, dtype=jnp.int32)
        W = jax.random.normal(k3, (D_OUT, D_IN), dtype=jnp.float32) / np.sqrt(D_IN)
        b_W = jnp.zeros((D_OUT,), dtype=jnp.float32)
        a_vec = jax.random.normal(k4, (2 * D_OUT,), dtype=jnp.float32) / np.sqrt(2 * D_OUT)
        b_a = jnp.zeros((1,), dtype=jnp.float32)
        return {'node_features': node_features, 'adjacency_matrix': adjacency_matrix, 'W': W, 'b_W': b_W, 'a_vec': a_vec, 'b_a': b_a}
    _L0_gnn_all = _L0_gnn_setup()
    _L0_gnn_in = {k: v for k, v in _L0_gnn_all.items() if k in ('W', 'b_W', 'a_vec', 'b_a')}
    del _L0_gnn_all

    def _L1_gnn_setup():
        import jax, jax.numpy as jnp
        import numpy as np
        N, IN_DIM, OUT_DIM = (4096, 128, 128)
        NEG_INF = -1000000000.0
        key = jax.random.key(seed)
        k1, k2, k3, k4 = jax.random.split(key, 4)
        X = jax.random.normal(k1, (N, IN_DIM), dtype=jnp.float32)
        A = jax.random.randint(k2, (N, N), 0, 2).astype(jnp.int32)
        W_fc = jax.random.normal(k3, (IN_DIM, OUT_DIM), dtype=jnp.float32) * (1.0 / np.sqrt(IN_DIM))
        b_fc = jnp.zeros((OUT_DIM,), dtype=jnp.float32)
        w_att = jax.random.normal(k4, (2 * OUT_DIM,), dtype=jnp.float32) * (1.0 / np.sqrt(2 * OUT_DIM))
        b_att = jnp.zeros((), dtype=jnp.float32)
        return {'X': X, 'A': A, 'W_fc': W_fc, 'b_fc': b_fc, 'w_att': w_att, 'b_att': b_att}
    _L1_gnn_all = _L1_gnn_setup()
    _L1_gnn_in = {k: v for k, v in _L1_gnn_all.items() if k in ('W_fc', 'b_fc', 'w_att', 'b_att')}
    del _L1_gnn_all
    return {'x': x, 'adj': adj, 'L0_gnn_W': _L0_gnn_in['W'], 'L0_gnn_b_W': _L0_gnn_in['b_W'], 'L0_gnn_a_vec': _L0_gnn_in['a_vec'], 'L0_gnn_b_a': _L0_gnn_in['b_a'], 'L1_gnn_W_fc': _L1_gnn_in['W_fc'], 'L1_gnn_b_fc': _L1_gnn_in['b_fc'], 'L1_gnn_w_att': _L1_gnn_in['w_att'], 'L1_gnn_b_att': _L1_gnn_in['b_att']}

def reference(x, adj, L0_gnn_W, L0_gnn_b_W, L0_gnn_a_vec, L0_gnn_b_a, L1_gnn_W_fc, L1_gnn_b_fc, L1_gnn_w_att, L1_gnn_b_att):
    import jax
    import jax.numpy as jnp

    def _L0_gnn_ref(node_features, adjacency_matrix, W, b_W, a_vec, b_a):
        import jax, jax.numpy as jnp
        import numpy as np
        N = 4096
        D_IN = 128
        D_OUT = 128
        NEG_INF = -9000000000000000.0
        h = node_features @ W.T + b_W
        a1, a2 = (a_vec[:D_OUT], a_vec[D_OUT:])
        e = (h @ a1)[:, None] + (h @ a2)[None, :] + b_a[0]
        e = jnp.where(e > 0, e, 0.2 * e)
        scores = jnp.where(adjacency_matrix > 0, e, jnp.float32(NEG_INF))
        attention = jax.nn.softmax(scores, axis=1)
        h_prime = attention @ h
        return h_prime

    def _L1_gnn_ref(X, A, W_fc, b_fc, w_att, b_att):
        import jax, jax.numpy as jnp
        import numpy as np
        N, IN_DIM, OUT_DIM = (4096, 128, 128)
        NEG_INF = -1000000000.0
        H = X @ W_fc + b_fc
        d = H.shape[1]
        s_src = H @ w_att[:d]
        s_dst = H @ w_att[d:]
        scores = s_src[:, None] + s_dst[None, :] + b_att
        scores = jnp.where(A > 0, scores, jnp.float32(NEG_INF))
        alpha = jax.nn.softmax(scores, axis=1)
        return alpha @ H
    x = _layernorm(x + _L0_gnn_ref(x, adj, L0_gnn_W, L0_gnn_b_W, L0_gnn_a_vec, L0_gnn_b_a), axis=-1)
    x = _layernorm(x + _L1_gnn_ref(x, adj, L1_gnn_W_fc, L1_gnn_b_fc, L1_gnn_w_att, L1_gnn_b_att), axis=-1)
    return x

_drawn_inputs = setup_inputs


def setup_inputs(seed=0):
    import zlib

    import numpy as np

    out = dict(_drawn_inputs(seed))
    spreads = {'L0_gnn_b_W': (0.0, 0.1), 'L1_gnn_b_fc': (0.0, 0.1)}
    factors = {}
    for name, (base, spread) in spreads.items():
        noise = np.random.default_rng([zlib.crc32(name.encode()), seed]).standard_normal(out[name].shape)
        drawn = base * np.exp(spread * noise) if base else spread * noise
        out[name] = jnp.asarray(drawn.astype(out[name].dtype))
    for name, factor in factors.items():
        out[name] = (out[name] * factor).astype(out[name].dtype)
    return out
```

```python
def build_two_layer_gat(nc, x, adj, w0t, b0, a12, ba, w1, b1, watt, packer, eye, out):
    import concourse.bass as bass
    from concourse import mybir
    from contextlib import ExitStack

    dt = mybir.dt
    F32, F16, F8, U8, U16, I32 = dt.float32, dt.float16, dt.float8e4, dt.uint8, dt.uint16, dt.int32
    ALU, ACT, AX = mybir.AluOpType, mybir.ActivationFunctionType, mybir.AxisListType
    MAX = bass.bass_isa.ReduceOp.max
    ds = bass.ds

    P = 128
    N, D = x.shape
    TILES = N // P
    QUARTERS = 4
    CH = N // QUARTERS
    JQ = CH // P
    JH = TILES // 2
    DIGITS = 4
    GROUP = P // DIGITS
    WORDS = GROUP // 2
    HALF = D + 1
    COLS = 2 * HALF
    XC = 512
    XT = XC // P
    CHUNKS = N // XC
    GJ = 8
    NG = TILES // GJ
    SLOPE = 0.2
    EPS = 1e-5
    LO = 2.0 ** 11
    TOP = 2.0 ** 25
    MASK = 0x4040
    NEG_BYTE = 47
    STEPS0 = 8

    adj_v = adj.rearrange("(t p) (q c) -> t p q c", p=P, q=QUARTERS)
    x_chunks = x.rearrange("(c k p) d -> c p k d", k=XT, p=P)
    x_tiles = x.rearrange("(t p) d -> t p d", p=P)
    out_tiles = out.rearrange("(t p) d -> t p d", p=P)
    words_dram = nc.dram_tensor("words_dram", (TILES, P, TILES * WORDS), U16, kind="Internal").ap()
    xh_dram = nc.dram_tensor("xh_dram", (TILES, P, 2 * D), F32, kind="Internal").ap()

    def row(dram, t):
        return dram[ds(t, 1)].rearrange("o p d -> p (o d)")

    ctx = ExitStack()
    with ctx:
        def sb(name, shape, dtype):
            return ctx.enter_context(nc.sbuf_tensor(name, shape, dtype))

        def pb(name, shape, dtype):
            return ctx.enter_context(nc.psum_tensor(name, shape, dtype))

        def sem(name):
            return ctx.enter_context(nc.semaphore(name))

        s2_row = sb("s2_row", [P, N], F32)
        wts_pos = sb("wts_pos", [P, TILES, COLS], F16)
        wts_neg = sb("wts_neg", [P, TILES, COLS], F16)
        adj_in = sb("adj_in", [P, QUARTERS, CH], I32)
        h1_all = adj_in[:, :, :].rearrange("p q c -> p (q c)").bitcast(F32).rearrange("p (t d) -> p t d", d=D)
        present = sb("present", [P, QUARTERS, CH], U8)
        words_in = present[:, :, :].rearrange("p q c -> p (q c)").bitcast(U16).rearrange(
            "p (s w) -> p s w", w=TILES * WORDS)
        branch = sb("branch", [P, QUARTERS, CH], U8)
        words = sb("words", [P, 2, TILES, WORDS], U16)
        masks = sb("masks", [P, 2, 2, TILES, P], U8)
        h_all = masks[:, :, :, :, :].rearrange("p a b t i -> p (a b t i)").bitcast(F32).rearrange(
            "p (t d) -> p t d", d=D)
        scratch = sb("scratch", [P, 2, GJ * D], F32)
        xT_sb = scratch[:, :, 0:XC]
        hT_sb = scratch[:, :, XC:2 * XC]
        acc = sb("acc", [P, 2, 2 * COLS], F32)
        x_in = acc[:, :, :].rearrange("p a c -> p (a c)")[:, 0:2 * XC].rearrange(
            "p (b k d) -> p b k d", b=2, k=XT)
        x_res = sb("x_res", [P, 2, D], F32)
        xh = sb("xh", [P, 2, 2 * D], F32)
        total = sb("total", [P, COLS], F32)
        num = sb("num", [P, HALF], F32)
        guarded = sb("guarded", [P, HALF], F32)
        pre = sb("pre", [P, 2, D], F32)
        x1T_sb = sb("x1T_sb", [P, P], F32)
        w0t_sb = sb("w0t_sb", [P, D], F32)
        w1_sb = sb("w1_sb", [P, D], F32)
        eye_sb = sb("eye_sb", [P, P], F32)
        a2_rep = sb("a2_rep", [P, P], F32)
        ones = a2_rep
        diag = x1T_sb
        b1_row = sb("b1_row", [P, D], F32)
        wdst_row = sb("wdst_row", [P, D], F32)
        mean_row = sb("mean_row", [P, HALF], F32)
        hsum = sb("hsum", [P, D], F32)
        packer_sb = sb("packer_sb", [P, WORDS], dt.bfloat16)
        a12_sb = sb("a12_sb", [P, 2], F32)
        b0_sb = sb("b0_sb", [P, 1], F32)
        ba_sb = sb("ba_sb", [P, 1], F32)
        s12 = sb("s12", [P, TILES, 2], F32)
        s_dst = sb("s_dst", [P, TILES], F32)
        thr = sb("thr", [P, TILES], F32)
        zM = sb("zM", [P, TILES], F32)
        zlow = sb("zlow", [P, TILES], F32)
        alpha = sb("alpha", [P, TILES], F32)
        beta = sb("beta", [P, TILES], F32)
        v = sb("v", [P, 2, TILES], F32)
        vK = sb("vK", [P, 2, TILES], F32)
        vD = sb("vD", [P, 2, TILES], F32)
        chunk_stats = sb("chunk_stats", [P, 3, CHUNKS], F32)
        hmax_t = sb("hmax_t", [P, TILES], F32)
        cst = sb("cst", [P, 10], F32)
        sig_bias = sb("sig_bias", [P, 1], F32)
        eps = sb("eps", [P, 1], F32)
        minus_half = sb("minus_half", [P, 1], F32)
        iszero = sb("iszero", [P, 1], F32)
        rden = sb("rden", [P, 2], F32)
        bn = sb("bn", [P, 6], F32)
        mv = sb("mv", [P, 2, 2], F32)
        veps = sb("veps", [P, 1], F32)
        rstd = sb("rstd", [P, 2], F32)

        bank = [pb(f"bank{i}", [P, 512], F32) for i in range(8)]
        acc_ps = [(bank[0], bank[1]), (bank[2], bank[3])]
        pack_ps = [bank[4], bank[5]]
        x1T_ps, h1_ps = bank[6], bank[7]
        xT_ps, hT_ps, s2_ps, hn_ps, s12_ps = bank[0:2], bank[2:4], bank[4], bank[5], bank[6]

        const_in = sem("const_in")
        dve_const = sem("dve_const")
        x_in_landed = [sem("x_in_landed0"), sem("x_in_landed1")]
        xT_done, xT_copied = sem("xT_done"), sem("xT_copied")
        hT_done, hT_copied = sem("hT_done"), sem("hT_copied")
        hT_maxed = sem("hT_maxed")
        s2_done, s2_copied = sem("s2_done"), sem("s2_copied")
        hn_done, hn_copied = sem("hn_done"), sem("hn_copied")
        setup = sem("setup")
        hmax_in, hmax_out = sem("hmax_in"), sem("hmax_out")
        diag_ready, hsum_done = sem("diag_ready"), sem("hsum_done")
        exp_in, exp_out = sem("exp_in"), sem("exp_out")
        vk_ready = sem("vk_ready")
        y_pos, y_neg = sem("y_pos"), sem("y_neg")
        hi_pos, hi_neg = sem("hi_pos"), sem("hi_neg")
        lo_pos, lo_neg = sem("lo_pos"), sem("lo_neg")
        den_step = sem("den_step")
        adj_landed = [sem(f"adj_landed{q}") for q in range(QUARTERS)]
        present_made, branch_made, edges_made = sem("present_made"), sem("branch_made"), sem("edges_made")
        packed, words_made = sem("packed"), sem("words_made")
        words_stored = [sem("words_stored0"), sem("words_stored1")]
        masks_made, acc_done, acc_copied = sem("masks_made"), sem("acc_done"), sem("acc_copied")
        x_res_landed = [sem("x_res_landed0"), sem("x_res_landed1")]
        fold, stats_made, veps_made, rstd_made = sem("fold"), sem("stats_made"), sem("veps_made"), sem("rstd_made")
        x1_made, x1T_done, x1T_copied, h1_done = sem("x1_made"), sem("x1T_done"), sem("x1T_copied"), sem("h1_done")
        h1_biased, h1_made, hsum_added = sem("h1_biased"), sem("h1_made"), sem("hsum_added")
        xh_stored = [sem("xh_stored0"), sem("xh_stored1")]
        h1_in = [sem(f"h1_in{g}") for g in range(NG)]
        max1_in, max1_out = sem("max1_in"), sem("max1_out")
        y1, hi1, lo1 = sem("y1"), sem("hi1"), sem("lo1")
        words_landed = [sem("words_landed0"), sem("words_landed1")]
        any_made, masks1_made, acc1_done, acc1_copied = sem("any_made"), sem("masks1_made"), sem("acc1_done"), sem("acc1_copied")
        x1_landed = [sem("x1_landed0"), sem("x1_landed1")]
        fold1, stats1, veps1, rstd1, out_made = sem("fold1"), sem("stats1"), sem("veps1"), sem("rstd1"), sem("out_made")
        out_stored = [sem("out_stored0"), sem("out_stored1")]

        act_passed, dve_passed, pe_passed = sem("act_passed"), sem("dve_passed"), sem("pe_passed")

        block = ctx.enter_context(nc.Block())
        CONSTS = 11

        @block.sync
        def _(sp):
            for dst, src in (
                (eye_sb[:, :], eye), (w0t_sb[:, :], w0t), (a12_sb[:, :], a12),
                (b0_sb[:, :], b0), (ba_sb[:, :], ba.to_broadcast([P, 1])),
                (packer_sb[:, :], packer), (w1_sb[:, :], w1),
                (b1_row[:, :], b1.to_broadcast([P, D])), (wdst_row[:, :], watt[:, D:2 * D].to_broadcast([P, D])),
            ):
                sp.dma_start(dst, src).then_inc(const_in, 16)
            for b in range(2):
                sp.dma_start(x_in[:, b], x_chunks[b]).then_inc(x_in_landed[b], 16)
            with sp.Fori(1, CHUNKS // 2) as u:
                for b in range(2):
                    sp.wait_ge(xT_done, 2 * u + b - 1)
                    sp.dma_start(x_in[:, b], x_chunks[ds(2 * u + b, 1)].rearrange(
                        "o p k d -> p (o k) d")).then_inc(x_in_landed[b], 16)

            def feed(t):
                for q in range(QUARTERS):
                    sp.wait_ge(present_made, 4 * (t - 1) + q + 1)
                    sp.dma_start(adj_in[:, q, :], adj_v[ds(t, 1), :, q, :].rearrange(
                        "o p c -> p (o c)")).then_inc(adj_landed[q], 16)

            def residual(t, b, first=False):
                if not first:
                    sp.wait_ge(fold, STEPS0 * (t - 1))
                sp.dma_start(x_res[:, b, :], row(x_tiles, t)).then_inc(x_res_landed[b], 16)

            def store_words(t, b):
                sp.wait_ge(words_made, 2 * t + 2)
                sp.dma_start(row(words_dram, t), words[:, b].rearrange("p t w -> p (t w)")).then_inc(
                    words_stored[b], 16)

            def store_xh(t, b):
                sp.wait_ge(h1_made, t + 1)
                sp.dma_start(row(xh_dram, t), xh[:, b, :]).then_inc(xh_stored[b], 16)

            feed(1)
            feed(2)
            store_words(0, 0)
            for t in range(2):
                residual(t, t, first=True)
                feed(t + 3)
                store_words(t + 1, (t + 1) % 2)
            with sp.Fori(0, (TILES - 6) // 2) as u:
                for k in range(2):
                    t = 2 * u + k + 2
                    residual(t, k)
                    store_xh(t - 2, k)
                    feed(t + 3)
                    store_words(t + 1, 1 - k)
            for t in range(TILES - 4, TILES):
                residual(t, t % 2)
                store_xh(t - 2, t % 2)
                if t + 3 < TILES:
                    feed(t + 3)
                if t + 1 < TILES:
                    store_words(t + 1, (t + 1) % 2)
            sp.wait_ge(present_made, 4 * TILES)

            def load_h1(g):
                sp.dma_start(h1_all[:, GJ * g:GJ * (g + 1), :],
                             xh_dram[GJ * g:GJ * (g + 1), :, D:2 * D].rearrange("t p d -> p t d")).then_inc(
                    h1_in[g], 16)

            sp.wait_ge(xh_stored[0], 16 * (JH - 1))
            sp.wait_ge(xh_stored[1], 16 * (JH - 1))
            for g in range(NG - 1):
                load_h1(g)
            for b in range(2):
                sp.wait_ge(words_stored[b], 16 * JH)
            sp.wait_ge(edges_made, 4 * TILES)

            def load_words(t, b, first=False):
                if not first:
                    sp.wait_ge(any_made, t - 1)
                sp.dma_start(words_in[:, b, :], row(words_dram, t)).then_inc(words_landed[b], 16)

            def load_x1(t, b, first=False):
                if first:
                    sp.wait_ge(fold, STEPS0 * (TILES - 1 + b))
                else:
                    sp.wait_ge(fold1, 7 * (t - 1))
                sp.dma_start(x_res[:, b, :], xh_dram[ds(t, 1), :, 0:D].rearrange(
                    "o p d -> p (o d)")).then_inc(x1_landed[b], 16)

            def store_out(t, b):
                sp.wait_ge(out_made, t + 1)
                sp.dma_start(row(out_tiles, t), xh[:, b, 0:D]).then_inc(out_stored[b], 16)

            for t in range(2):
                load_words(t, t, first=True)
            for t in range(TILES - 2, TILES):
                store_xh(t, t % 2)
            for b in range(2):
                sp.wait_ge(xh_stored[b], 16 * JH)
            load_h1(NG - 1)
            for t in range(2):
                load_x1(t, t, first=True)
            for t in (0, 1):
                load_words(t + 2, t)
            with sp.Fori(0, (TILES - 4) // 2) as u:
                for b in range(2):
                    t = 2 * u + b + 2
                    load_words(t + 2, b)
                    load_x1(t, b)
                    store_out(t - 2, b)
            for t in range(TILES - 2, TILES):
                load_x1(t, t % 2)
                store_out(t - 2, t % 2)
            for t in range(TILES - 2, TILES):
                store_out(t, t % 2)
            for b in range(2):
                sp.wait_ge(out_stored[b], 16 * JH)

        @block.scalar
        def _(act):
            for q in range(QUARTERS):
                act.dma_start(adj_in[:, q, :], adj_v[0, :, q, :]).then_inc(adj_landed[q], 16)
            act.wait_ge(const_in, 16 * (CONSTS - 2))

            def copy_xT(c, b):
                act.wait_ge(xT_done, c + 1)
                nc.scalar.copy(xT_sb[:, b, :], xT_ps[b][:, :]).then_inc(xT_copied, 1)

            def copy_hT(c, b):
                act.wait_ge(hT_done, c + 1)
                nc.scalar.activation(hT_sb[:, b, :], hT_ps[b][:, :], ACT.Identity, bias=b0_sb[:, 0:1],
                                     accum_out=chunk_stats[:, 2, ds(c, 1)]).then_inc(hT_copied, 1)

            copy_xT(0, 0)
            with act.Fori(0, (CHUNKS - 2) // 2) as u:
                for k in range(2):
                    copy_xT(2 * u + k + 1, 1 - k)
                    copy_hT(2 * u + k, k)
            copy_xT(CHUNKS - 1, 1)
            copy_hT(CHUNKS - 2, 0)
            act.wait_ge(hn_done, CHUNKS - 2)
            copy_hT(CHUNKS - 1, 1)

            act.wait_ge(exp_in, 1)
            nc.scalar.activation(v[:, 0, :], s12[:, :, 1], ACT.Exp, bias=cst[:, 3:4])
            nc.scalar.activation(v[:, 1, :], s12[:, :, 1], ACT.Exp, bias=cst[:, 4:5], scale=SLOPE)
            nc.scalar.activation(alpha[:, :], zM[:, :], ACT.Exp)
            nc.scalar.activation(beta[:, :], zlow[:, :], ACT.Exp).then_inc(exp_out, 1)

            def make_present(t, q, nth):
                act.wait_ge(adj_landed[q], 16 * t + 16)
                if nth:
                    act.wait_ge(edges_made, 4 * t - 4 + q + 1)
                act.sem_inc(act_passed, 1)
                nc.scalar.activation(present[:, q, :].bitcast(F8), adj_in[:, q, :], ACT.Sigmoid,
                                     bias=sig_bias[:, 0:1], scale=64.0, saturate=False).then_inc(present_made, 1)

            def copy_words(t, b, half, free=None):
                act.wait_ge(packed, 4 * t + 2 * half + 2)
                if free is not None:
                    act.wait_ge(masks_made, t - 1)
                    act.wait_ge(words_stored[b], 16 * free)
                nc.scalar.copy(words[:, b, half * JH:(half + 1) * JH, :],
                               pack_ps[half][:, 0:JH * WORDS].rearrange("p (j w) -> p j w", w=WORDS)).then_inc(
                    words_made, 1)

            def copy_acc(t, b, older=True):
                act.wait_ge(acc_done, t + 1)
                if older:
                    act.wait_ge(fold, STEPS0 * (t - 2) + 1 if not isinstance(t, int) or t > 1 else 1)
                nc.scalar.mul(acc[:, b, 0:COLS], acc_ps[b][0][:, 0:COLS], alpha[:, ds(t, 1)])
                nc.scalar.mul(acc[:, b, COLS:2 * COLS], acc_ps[b][1][:, 0:COLS], beta[:, ds(t, 1)]).then_inc(
                    acc_copied, 1)

            def copy_x1T(t):
                act.wait_ge(x1T_done, t + 1)
                nc.scalar.copy(x1T_sb[:, :], x1T_ps[:, 0:P]).then_inc(x1T_copied, 1)

            def hi_halves(g, pos, neg):
                for made, kind, wts, done in ((y_pos, 0, wts_pos, hi_pos), (y_neg, 1, wts_neg, hi_neg)):
                    act.wait_ge(made, g + 1)
                    nc.scalar.mul(wts[:, GJ * g:GJ * (g + 1), 0:D],
                                  scratch[:, kind, :].rearrange("p (j d) -> p j d", d=D), 1.0 / LO).then_inc(done, 1)

            early = NG // 2
            for g in range(early):
                hi_halves(g, None, None)
                for q in range(QUARTERS * g // early, QUARTERS * (g + 1) // early):
                    make_present(0, q, 0)
            copy_words(0, 0, 0)
            copy_words(0, 0, 1)
            for g in range(early, NG):
                hi_halves(g, None, None)
            for q in range(QUARTERS):
                make_present(1, q, 1)
            make_present(2, 0, 1)
            copy_words(1, 1, 0)
            make_present(2, 1, 1)
            copy_words(1, 1, 1)
            make_present(2, 2, 1)
            make_present(2, 3, 1)

            def iteration(t, b, free, last=False, older=True):
                copy_acc(t - 1, 1 - b, older)
                if not last:
                    make_present(t + 2, 0, 1)
                copy_words(t + 1, 1 - b, 0, free)
                if not last:
                    make_present(t + 2, 1, 1)
                copy_words(t + 1, 1 - b, 1, free)
                copy_x1T(t - 1)
                if not last:
                    make_present(t + 2, 2, 1)
                    make_present(t + 2, 3, 1)

            iteration(1, 1, 1, older=False)
            iteration(2, 0, 1, older=False)
            with act.Fori(0, (TILES - 6) // 2) as u:
                for k in range(2):
                    t = 2 * u + k + 3
                    iteration(t, 1 - k, u + 2)
            iteration(TILES - 3, 1, JH - 1)
            iteration(TILES - 2, 0, JH - 1, last=True)
            copy_acc(TILES - 2, 0)
            copy_x1T(TILES - 2)
            copy_acc(TILES - 1, 1)
            copy_x1T(TILES - 1)

            act.wait_ge(max1_out, 3)
            nc.scalar.activation(v[:, 0, :], s_dst[:, :], ACT.Exp, bias=cst[:, 3:4]).then_inc(exp_out, 1)
            for g in range(NG):
                act.wait_ge(y1, g + 1)
                nc.scalar.mul(wts_pos[:, GJ * g:GJ * (g + 1), 0:D],
                              scratch[:, g % 2, :].rearrange("p (j d) -> p j d", d=D), 1.0 / LO).then_inc(hi1, 1)

            def copy_acc1(t, b, older=True):
                act.wait_ge(acc1_done, t + 1)
                if older:
                    act.wait_ge(fold1, 7 * (t - 2) + 1)
                nc.scalar.copy(acc[:, b, 0:COLS], acc_ps[b][0][:, 0:COLS]).then_inc(acc1_copied, 1)

            copy_acc1(0, 0, older=False)
            copy_acc1(1, 1, older=False)
            with act.Fori(1, JH) as u:
                for b in range(2):
                    copy_acc1(2 * u + b, b)

        @block.vector
        def _(dve):
            nc.vector.memset(sig_bias[:, :], -32.0)
            nc.vector.memset(minus_half[:, :], -0.5)
            nc.vector.memset(eps[:, :], EPS)
            dve.wait_ge(const_in, 16 * (CONSTS - 2))
            nc.vector.tensor_copy(a2_rep[:, :], a12_sb[:, 1:2].to_broadcast([P, P])).then_inc(dve_const, 1)

            def chunk_out(c, b):
                dve.wait_ge(hT_copied, c + 1)
                nc.vector.tensor_reduce(chunk_stats[:, 1, ds(c, 1)], hT_ps[b][:, :], AX.X, ALU.max,
                                        apply_absolute_value=True).then_inc(hT_maxed, 1)
                dve.wait_ge(s2_done, c + 1)
                nc.vector.tensor_copy(s2_row[:, ds(c * XC, XC)], s2_ps[:, :])
                nc.vector.tensor_copy(s12[:, ds(c * XT, XT), :],
                                      s12_ps[:, 0:2 * XT].rearrange("p (k s) -> p k s", s=2))
                nc.vector.tensor_reduce(chunk_stats[:, 0, ds(c, 1)], s2_ps[:, :], AX.X, ALU.max).then_inc(s2_copied, 1)
                dve.wait_ge(hn_done, c + 1)
                nc.vector.tensor_copy(h_all[:, ds(c * XT, XT), :],
                                      hn_ps[:, :].rearrange("p (k d) -> p k d", d=D)).then_inc(hn_copied, 1)

            with dve.Fori(0, CHUNKS // 2) as u:
                for b in range(2):
                    chunk_out(2 * u + b, b)

            steps = [0]

            def step(ins):
                steps[0] += 1
                ins.then_inc(setup, 1)
                dve.wait_ge(setup, steps[0])

            dve.wait_ge(hn_copied, CHUNKS)
            nc.vector.tensor_reduce(cst[:, 1:2], chunk_stats[:, 1, :], AX.X, ALU.max).then_inc(hmax_in, 1)
            nc.vector.tensor_reduce(cst[:, 2:3], chunk_stats[:, 2, :], AX.X, ALU.add)
            step(nc.vector.tensor_reduce(cst[:, 0:1], chunk_stats[:, 0, :], AX.X, ALU.max))
            nc.vector.tensor_scalar(diag[:, :], eye_sb[:, :], cst[:, 2:3], None, ALU.mult)
            nc.vector.memset(ones[:, :], 1.0).then_inc(diag_ready, 1)
            nc.vector.tensor_scalar(cst[:, 3:4], cst[:, 0:1], -1.0, None, ALU.mult)
            nc.vector.tensor_scalar(cst[:, 4:5], cst[:, 0:1], -SLOPE, None, ALU.mult)
            nc.vector.tensor_scalar(thr[:, :], s12[:, :, 0], ba_sb[:, 0:1], -1.0, ALU.add, ALU.mult)
            step(nc.vector.tensor_scalar(zM[:, :], s12[:, :, 0], ba_sb[:, 0:1], cst[:, 0:1], ALU.add, ALU.add))
            step(nc.vector.scalar_tensor_tensor(zlow[:, :], zM[:, :], SLOPE, zM[:, :], ALU.mult, ALU.max))
            step(nc.vector.tensor_tensor(alpha[:, :], zM[:, :], zlow[:, :], ALU.subtract))
            step(nc.vector.scalar_tensor_tensor(zlow[:, :], zM[:, :], SLOPE, zlow[:, :], ALU.mult, ALU.subtract))
            nc.vector.tensor_copy(zM[:, :], alpha[:, :]).then_inc(exp_in, 1)

            def scales(layer_done):
                step(nc.vector.tensor_scalar(cst[:, 5:6], cst[:, 1:2], 1e-30, None, ALU.max))
                step(nc.vector.tensor_scalar(cst[:, 5:6].bitcast(I32), cst[:, 5:6].bitcast(I32), 0x7F800000,
                                             None, ALU.bitwise_and))
                step(nc.vector.reciprocal(cst[:, 6:7], cst[:, 5:6]))
                nc.vector.tensor_scalar(cst[:, 8:9], cst[:, 6:7], 1.0 / N, None, ALU.mult)
                step(nc.vector.tensor_scalar(cst[:, 7:8], cst[:, 6:7], TOP, None, ALU.mult))

            def mean_of_h(nth):
                dve.wait_ge(hsum_done, nth)
                nc.vector.tensor_scalar(mean_row[:, 0:D], x1T_ps[:, 0:D] if nth == 1 else h1_ps[:, 0:D],
                                        cst[:, 8:9], None, ALU.mult)

            def denominators(kinds, nth):
                for kind, wts in kinds:
                    nc.vector.tensor_scalar(vK[:, kind, :], v[:, kind, :], cst[:, 7:8], None, ALU.mult)
                    step(nc.vector.tensor_scalar(vD[:, kind, :], v[:, kind, :], TOP, None, ALU.mult))
                    step(nc.vector.tensor_scalar(wts[:, :, D], vD[:, kind, :], 1.0 / LO, None, ALU.mult))
                    nc.vector.scalar_tensor_tensor(wts[:, :, COLS - 1], wts[:, :, D], -LO, vD[:, kind, :],
                                                   ALU.mult, ALU.add).then_inc(den_step, 1)

            dve.wait_ge(hmax_out, 1)
            scales(0)
            mean_of_h(1)
            nc.vector.memset(mean_row[:, D:HALF], 1.0)
            dve.wait_ge(exp_out, 1)
            denominators(((0, wts_pos), (1, wts_neg)), 0)
            dve.wait_ge(den_step, 2)

            def product(kind, g, src):
                return nc.vector.tensor_tensor(
                    scratch[:, kind % 2, :].rearrange("p (j d) -> p j d", d=D), src[:, GJ * g:GJ * (g + 1), :],
                    vK[:, kind if src is h_all else 0, GJ * g:GJ * (g + 1)].unsqueeze(2).to_broadcast([P, GJ, D]),
                    ALU.mult)

            def low_half(wts, kind, g):
                return nc.vector.scalar_tensor_tensor(
                    wts[:, GJ * g:GJ * (g + 1), HALF:HALF + D], wts[:, GJ * g:GJ * (g + 1), 0:D], -LO,
                    scratch[:, kind, :].rearrange("p (j d) -> p j d", d=D), ALU.mult, ALU.add)

            def make_branch(t, q, older=True):
                if older:
                    dve.wait_ge(packed, 4 * t - 4 + q + 1)
                nc.vector.tensor_scalar(branch[:, q, :], s2_row[:, q * CH:(q + 1) * CH],
                                        thr[:, ds(t, 1)], NEG_BYTE, ALU.is_gt, ALU.add).then_inc(
                    branch_made, 1)

            def make_edges(t, q):
                dve.wait_ge(branch_made, 4 * t + q + 1)
                dve.wait_ge(present_made, 4 * t + q + 1)
                nc.vector.tensor_tensor(branch[:, q, :].bitcast(U16), branch[:, q, :].bitcast(U16),
                                        present[:, q, :].bitcast(U16), ALU.bitwise_and).then_inc(edges_made, 1)

            def pieces(t):
                make_branch(t, 0)
                for q in range(1, QUARTERS):
                    make_branch(t, q)
                    make_edges(t, q - 1)
                make_edges(t, QUARTERS - 1)

            def unpack(src, dst, odd):
                to = dst.bitcast(U16)
                for k in range(DIGITS):
                    left = 6 - 2 * k - odd
                    last = nc.vector.tensor_scalar(
                        to[:, :, WORDS * k:WORDS * (k + 1)], src, abs(left), MASK,
                        ALU.logical_shift_left if left >= 0 else ALU.logical_shift_right, ALU.bitwise_and)
                return last

            def make_masks(t, b, older=True):
                dve.wait_ge(words_made, 2 * t + 2)
                if older:
                    dve.wait_ge(acc_done, t - 1)
                unpack(words[:, b], masks[:, b, 1], 0)
                unpack(words[:, b], masks[:, b, 0], 1).then_inc(masks_made, 1)

            def fold_tile(done, t, b, two_branches, copied, landed, nth, stats):
                n = [0]
                count = STEPS0 if two_branches else STEPS0 - 1

                def chained(ins):
                    n[0] += 1
                    ins.then_inc(done, 1)
                    dve.wait_ge(done, count * t + n[0])

                dve.wait_ge(copied, t + 1)
                src = acc[:, b, 0:COLS]
                if two_branches:
                    chained(nc.vector.tensor_tensor(total[:, :], acc[:, b, 0:COLS], acc[:, b, COLS:2 * COLS], ALU.add))
                    src = total[:, :]
                chained(nc.vector.scalar_tensor_tensor(num[:, :], src[:, HALF:COLS], 1.0 / LO, src[:, 0:HALF],
                                                       ALU.mult, ALU.add))
                chained(nc.vector.tensor_scalar(iszero[:, :], num[:, D:HALF], 0.0, None, ALU.is_equal))
                chained(nc.vector.scalar_tensor_tensor(guarded[:, :], mean_row[:, :], iszero[:, 0:1], num[:, :],
                                                       ALU.mult, ALU.add))
                chained(nc.vector.reciprocal(rden[:, 0:1], guarded[:, D:HALF]))
                chained(nc.vector.tensor_scalar(rden[:, 1:2], rden[:, 0:1], cst[:, 5:6], None, ALU.mult))
                dve.wait_ge(landed, nth)
                chained(nc.vector.scalar_tensor_tensor(pre[:, b, :], guarded[:, 0:D], rden[:, 1:2], x_res[:, b, :],
                                                       ALU.mult, ALU.add))
                chained(nc.vector.bn_stats(bn[:, :], pre[:, b, :]))
                dve.sem_inc(dve_passed, 1)
                nc.vector.bn_aggr(mv[:, b, :], bn[:, :]).then_inc(stats, 1)

            def normalise(t, b, ready, made, stored, nth):
                dve.wait_ge(ready, t + 1)
                if nth is not None:
                    dve.wait_ge(stored, nth)
                nc.vector.tensor_scalar(xh[:, b, 0:D], pre[:, b, :], mv[:, b, 0:1], rstd[:, b:b + 1],
                                        ALU.subtract, ALU.mult).then_inc(made, 1)

            def finish_h1(t, b, older=True):
                dve.wait_ge(h1_done, t + 1)
                if older:
                    dve.wait_ge(hsum_added, t)
                nc.vector.tensor_tensor(xh[:, b, D:2 * D], h1_ps[:, 0:D], b1_row[:, :], ALU.add).then_inc(h1_biased, 1)
                dve.wait_ge(h1_biased, t + 1)
                nc.vector.scalar_tensor_tensor(num[:, 0:D], xh[:, b, D:2 * D], 1.0, wdst_row[:, :], ALU.mult,
                                               ALU.mult, accum_out=s_dst[:, ds(t, 1)])
                nc.vector.tensor_reduce(hmax_t[:, ds(t, 1)], xh[:, b, D:2 * D], AX.X, ALU.max,
                                        apply_absolute_value=True).then_inc(h1_made, 1)

            early = NG // 2
            for g in range(NG):
                if g >= 1:
                    dve.wait_ge(hi_pos, g)
                    dve.wait_ge(lo_pos, g)
                product(0, g, h_all).then_inc(y_pos, 1)
                if g < early:
                    for q in range(QUARTERS * g // early, QUARTERS * (g + 1) // early):
                        make_branch(0, q, older=False)
                        make_edges(0, q)
                for kind, wts, hi, made, lo in ((0, wts_pos, hi_pos, y_pos, lo_pos), (1, wts_neg, hi_neg, y_neg, lo_neg)):
                    dve.wait_ge(made, g + 1)
                    dve.wait_ge(hi, g + 1)
                    low_half(wts, kind, g).then_inc(lo, 1)
                if g == early - 1:
                    make_masks(0, 0, older=False)
            pieces(1)
            make_masks(1, 1, older=False)

            def iteration(t, b, nth, last=False):
                if not last:
                    pieces(t + 1)
                fold_tile(fold, t - 1, 1 - b, True, acc_copied, x_res_landed[1 - b], 16 * nth, stats_made)
                if not isinstance(t, int) or t >= 2:
                    finish_h1(t - 2, b, older=not isinstance(t, int) or t >= 3)
                normalise(t - 1, 1 - b, rstd_made, x1_made, xh_stored[1 - b],
                          None if isinstance(t, int) and t < 3 else 16 * (nth - 1))
                if not last:
                    make_masks(t + 1, 1 - b)

            for t in (1, 2):
                iteration(t, t % 2, (t - 1) // 2 + 1)
            with dve.Fori(0, (TILES - 4) // 2) as u:
                for k in range(2):
                    iteration(2 * u + k + 3, 1 - k, u + 2)
            iteration(TILES - 1, 1, JH, last=True)
            fold_tile(fold, TILES - 1, 1, True, acc_copied, x_res_landed[1], 16 * JH, stats_made)
            finish_h1(TILES - 2, 0)
            normalise(TILES - 1, 1, rstd_made, x1_made, xh_stored[1], 16 * (JH - 1))
            finish_h1(TILES - 1, 1)

            dve.wait_ge(h1_made, TILES)
            nc.vector.tensor_reduce(cst[:, 0:1], s_dst[:, :], AX.X, ALU.max)
            nc.vector.tensor_reduce(cst[:, 1:2], hmax_t[:, :], AX.X, ALU.max).then_inc(max1_in, 1)
            dve.wait_ge(max1_out, 1)
            nc.vector.tensor_scalar(cst[:, 3:4], cst[:, 0:1], -1.0, None, ALU.mult).then_inc(max1_out, 2)
            scales(1)
            mean_of_h(2)
            dve.wait_ge(exp_out, 2)
            dve.wait_ge(acc_done, TILES)
            denominators(((0, wts_pos),), 1)
            dve.wait_ge(den_step, 3)

            def make_masks1(t, b, older=True, nth=None):
                dve.wait_ge(words_landed[b], nth)
                flat = words[:, b].rearrange("p t w -> p (t w)")
                nc.vector.scalar_tensor_tensor(flat, words_in[:, b, :], 1, words_in[:, b, :],
                                               ALU.logical_shift_right, ALU.bitwise_or).then_inc(any_made, 1)
                dve.wait_ge(any_made, t + 1)
                if older:
                    dve.wait_ge(acc1_done, t - 1)
                unpack(words[:, b], masks[:, b, 0], 0).then_inc(masks1_made, 1)

            make_masks1(0, 0, older=False, nth=16)
            for g in range(NG):
                dve.wait_ge(h1_in[g], 16)
                if g >= 2:
                    dve.wait_ge(lo1, g - 1)
                product(g % 2, g, h1_all).then_inc(y1, 1)
                if g >= 1:
                    dve.wait_ge(hi1, g)
                    low_half(wts_pos, (g - 1) % 2, g - 1).then_inc(lo1, 1)
            dve.wait_ge(hi1, NG)
            low_half(wts_pos, (NG - 1) % 2, NG - 1).then_inc(lo1, 1)
            make_masks1(1, 1, older=False, nth=16)

            def iteration1(t, b, nth, nth_w, last=False, older=True):
                if not last:
                    make_masks1(t + 1, 1 - b, nth=nth_w)
                fold_tile(fold1, t - 1, 1 - b, False, acc1_copied, x1_landed[1 - b], 16 * nth, stats1)
                normalise(t - 1, 1 - b, rstd1, out_made, out_stored[1 - b], 16 * (nth - 1) if older else None)

            iteration1(1, 1, 1, 32, older=False)
            iteration1(2, 0, 1, 32, older=False)
            with dve.Fori(0, (TILES - 4) // 2) as u:
                for k in range(2):
                    iteration1(2 * u + k + 3, 1 - k, u + 2, 16 * u + 48)
            iteration1(TILES - 1, 1, JH, None, last=True)
            iteration1(TILES, 0, JH, None, last=True)

        @block.gpsimd
        def _(pool):
            nc.gpsimd.memset(hsum[:, :], 0.0)
            pool.wait_ge(hmax_in, 1)
            nc.gpsimd.partition_all_reduce(cst[:, 1:2], cst[:, 1:2], P, MAX).then_inc(hmax_out, 1)
            pool.wait_ge(den_step, 2)
            for g in range(NG):
                if g >= 1:
                    pool.wait_ge(lo_neg, g)
                nc.gpsimd.tensor_tensor(
                    scratch[:, 1, :].rearrange("p (j d) -> p j d", d=D), h_all[:, GJ * g:GJ * (g + 1), :],
                    vK[:, 1, GJ * g:GJ * (g + 1)].unsqueeze(2).to_broadcast([P, GJ, D]), ALU.mult).then_inc(y_neg, 1)

            def inverse_std(t, b, made, veps_s, done):
                pool.wait_ge(made, t + 1)
                nc.gpsimd.tensor_tensor(veps[:, :], mv[:, b, 1:2], eps[:, :], ALU.add).then_inc(veps_s, 1)
                pool.wait_ge(veps_s, t + 1)
                nc.gpsimd.tensor_tensor(rstd[:, b:b + 1], veps[:, :], minus_half[:, :], ALU.pow).then_inc(done, 1)

            def add_h(t, b):
                pool.wait_ge(h1_made, t + 1)
                nc.gpsimd.tensor_tensor(hsum[:, :], hsum[:, :], xh[:, b, D:2 * D], ALU.add).then_inc(hsum_added, 1)

            inverse_std(0, 0, stats_made, veps_made, rstd_made)
            with pool.Fori(0, (TILES - 2) // 2) as u:
                for k in range(2):
                    t = 2 * u + k + 1
                    inverse_std(t, 1 - k, stats_made, veps_made, rstd_made)
                    add_h(t - 1, k)
            inverse_std(TILES - 1, 1, stats_made, veps_made, rstd_made)
            add_h(TILES - 2, 0)
            add_h(TILES - 1, 1)
            pool.wait_ge(max1_in, 1)
            nc.gpsimd.partition_all_reduce(cst[:, 0:2], cst[:, 0:2], P, MAX).then_inc(max1_out, 1)
            with pool.Fori(0, JH) as u:
                for b in range(2):
                    inverse_std(2 * u + b, b, stats1, veps1, rstd1)

        @block.tensor
        def _(pe):
            pe.wait_ge(const_in, 16 * (CONSTS - 2))

            def transpose_x(c, b, nth, older=True):
                pe.wait_ge(x_in_landed[b], nth)
                if older:
                    pe.wait_ge(xT_copied, c - 1)
                for k in range(XT):
                    last = nc.tensor.transpose(xT_ps[b][:, k * P:(k + 1) * P], x_in[:, b, k, :], eye_sb[:, :])
                last.then_inc(xT_done, 1)

            def make_hT(c, b, older=True):
                pe.wait_ge(xT_copied, c + 1)
                if older:
                    pe.wait_ge(hT_maxed, c - 1)
                nc.tensor.matmul(hT_ps[b][:, :], w0t_sb[:, :], xT_sb[:, b, :], start=True, stop=True).then_inc(hT_done, 1)

            def finish_chunk(c, b, older=True):
                pe.wait_ge(hT_copied, c + 1)
                if older:
                    pe.wait_ge(s2_copied, c)
                nc.tensor.matmul(s2_ps[:, :], a2_rep[:, :], hT_sb[:, b, :], start=True, stop=True)
                for k in range(XT):
                    last = nc.tensor.matmul(s12_ps[:, 2 * k:2 * k + 2], hT_sb[:, b, k * P:(k + 1) * P], a12_sb[:, :],
                                            start=True, stop=True)
                last.then_inc(s2_done, 1)
                if older:
                    pe.wait_ge(hn_copied, c)
                for k in range(XT):
                    last = nc.tensor.transpose(hn_ps[:, k * P:(k + 1) * P], hT_sb[:, b, k * P:(k + 1) * P], eye_sb[:, :])
                last.then_inc(hn_done, 1)

            pe.wait_ge(dve_const, 1)
            transpose_x(0, 0, 16, older=False)
            transpose_x(1, 1, 16, older=False)
            make_hT(0, 0, older=False)
            transpose_x(2, 0, 32)
            make_hT(1, 1, older=False)
            finish_chunk(0, 0, older=False)
            with pe.Fori(0, (CHUNKS - 4) // 2) as u:
                for k in range(2):
                    c = 2 * u + k + 2
                    transpose_x(c + 1, 1 - k, 16 * u + 32 + 16 * k)
                    make_hT(c, k)
                    finish_chunk(c - 1, 1 - k)
            transpose_x(CHUNKS - 1, 1, 8 * CHUNKS)
            make_hT(CHUNKS - 2, 0)
            finish_chunk(CHUNKS - 3, 1)
            make_hT(CHUNKS - 1, 1)
            finish_chunk(CHUNKS - 2, 0)
            finish_chunk(CHUNKS - 1, 1)
            pe.wait_ge(diag_ready, 1)
            pe.wait_ge(s2_copied, CHUNKS)
            nc.tensor.matmul(x1T_ps[:, 0:D], ones[:, :], diag[:, :], start=True, stop=True).then_inc(hsum_done, 1)

            def pack(t, q, older=True):
                pe.wait_ge(edges_made, 4 * t + q + 1)
                if older:
                    pe.wait_ge(words_made, 2 * t - 2 + q // 2 + 1)
                pe.sem_inc(pe_passed, 1)
                for j in range(JQ * q, JQ * (q + 1)):
                    at = WORDS * (j % JH)
                    last = nc.tensor.matmul(pack_ps[j // JH][:, at:at + WORDS],
                                            branch[:, q, P * (j % JQ):P * (j % JQ) + P].bitcast(F8),
                                            packer_sb[:, :], start=True, stop=True)
                last.then_inc(packed, 1)

            def multiply(t, b, jobs=(), older=True, weights=False):
                pe.wait_ge(masks_made, t + 1)
                if older:
                    pe.wait_ge(acc_copied, t - 1)
                pe.sem_inc(pe_passed, 1)
                for j in range(TILES):
                    if weights and j % GJ == 0:
                        pe.wait_ge(lo_pos, j // GJ + 1)
                        pe.wait_ge(lo_neg, j // GJ + 1)
                    for kind, wts in ((1, wts_neg), (0, wts_pos)):
                        last = nc.tensor.matmul(acc_ps[b][kind][:, 0:COLS], masks[:, b, kind, j, :].bitcast(F8),
                                                wts[:, j, :], start=(j == 0), stop=(j == TILES - 1))
                    for at, job in jobs:
                        if j == at * TILES // 64:
                            job()
                last.then_inc(acc_done, 1)

            def transpose_x1(t, b):
                pe.wait_ge(x1_made, t + 1)
                nc.tensor.transpose(x1T_ps[:, 0:P], xh[:, b, 0:D], eye_sb[:, :]).then_inc(x1T_done, 1)

            def make_h1(t, older=True):
                pe.wait_ge(x1T_copied, t + 1)
                if older:
                    pe.wait_ge(h1_made, t)
                nc.tensor.matmul(h1_ps[:, 0:D], x1T_sb[:, :], w1_sb[:, :], start=True, stop=True).then_inc(h1_done, 1)

            def iteration(t, b, older=True, last=False, older_h=True):
                jobs = [(48, lambda: transpose_x1(t - 1, 1 - b)), (60, lambda: make_h1(t - 1, older_h))]
                if not last:
                    jobs += [(8 * (q + 1) + 2, lambda q=q: pack(t + 1, q)) for q in range(QUARTERS)]
                multiply(t, b, jobs, older)

            for q in range(QUARTERS):
                pack(0, q, older=False)
            multiply(0, 0, older=False, weights=True)
            for q in range(QUARTERS):
                pack(1, q)
            iteration(1, 1, older=False, older_h=False)
            iteration(2, 0)
            with pe.Fori(0, (TILES - 4) // 2) as u:
                for k in range(2):
                    iteration(2 * u + k + 3, 1 - k)
            iteration(TILES - 1, 1, last=True)
            transpose_x1(TILES - 1, 1)
            make_h1(TILES - 1)

            pe.wait_ge(hsum_added, TILES)
            pe.wait_ge(h1_made, TILES)
            nc.tensor.matmul(h1_ps[:, 0:D], ones[:, :], hsum[:, :], start=True, stop=True).then_inc(hsum_done, 1)

            def multiply1(t, b, older=True, weights=False):
                pe.wait_ge(masks1_made, t + 1)
                if older:
                    pe.wait_ge(acc1_copied, t - 1)
                pe.sem_inc(pe_passed, 1)
                for j in range(TILES):
                    if weights and j % GJ == 0:
                        pe.wait_ge(lo1, j // GJ + 1)
                    last = nc.tensor.matmul(acc_ps[b][0][:, 0:COLS], masks[:, b, 0, j, :].bitcast(F8),
                                            wts_pos[:, j, :], start=(j == 0), stop=(j == TILES - 1))
                last.then_inc(acc1_done, 1)

            multiply1(0, 0, older=False, weights=True)
            multiply1(1, 1, older=False)
            with pe.Fori(1, JH) as u:
                for b in range(2):
                    multiply1(2 * u + b, b)


def kernel(x, adj, L0_gnn_W, L0_gnn_b_W, L0_gnn_a_vec, L0_gnn_b_a, L1_gnn_W_fc, L1_gnn_b_fc, L1_gnn_w_att,
           L1_gnn_b_att):
    import ml_dtypes
    import numpy as np
    import concourse.bacc as bacc
    from concourse import mybir
    from concourse.bass_utils import run_bass_kernel_spmd

    i = np.arange(128)
    place = 4.0 * 4.0 ** (i // 32) * 256.0 ** (i % 2)
    packer = np.where((i % 32 // 2)[:, None] == np.arange(16)[None, :], place[:, None], 0.0).astype(ml_dtypes.bfloat16)
    arrays = {
        "x": x, "adj": adj, "w0t": np.asarray(L0_gnn_W).T, "b0": np.reshape(L0_gnn_b_W, (-1, 1)),
        "a12": np.reshape(L0_gnn_a_vec, (2, -1)).T, "ba": np.reshape(L0_gnn_b_a, (1, 1)),
        "w1": L1_gnn_W_fc, "b1": np.reshape(L1_gnn_b_fc, (1, -1)), "watt": np.reshape(L1_gnn_w_att, (1, -1)),
        "packer": packer, "eye": np.eye(128, dtype=np.float32),
    }
    arrays = {f"in_{name}": np.ascontiguousarray(a) for name, a in arrays.items()}
    nc = bacc.Bacc("TRN2", target_bir_lowering=False, num_devices=1)
    ins = [nc.dram_tensor(name, a.shape, mybir.dt.from_np(a.dtype), kind="ExternalInput").ap()
           for name, a in arrays.items()]
    out = nc.dram_tensor("out", x.shape, mybir.dt.float32, kind="ExternalOutput").ap()
    build_two_layer_gat(nc, *ins, out)
    return run_bass_kernel_spmd(nc, [arrays], core_ids=[0]).results[0]["out"]
```

```python
def build_two_layer_gat(nc, x, adj, w0, w0t, b0_col, b0, a12, ba, w1, b1, watt, packer, eye, out):
    import concourse.bass as bass
    from concourse import mybir
    from contextlib import ExitStack

    dt = mybir.dt
    F32, F16, F8, U8, U16, I32 = dt.float32, dt.float16, dt.float8e4, dt.uint8, dt.uint16, dt.int32
    ALU, ACT, AX = mybir.AluOpType, mybir.ActivationFunctionType, mybir.AxisListType
    MAX = bass.bass_isa.ReduceOp.max
    ds = bass.ds

    P = 128
    N, D = x.shape
    TILES = N // P
    QUARTERS = 4
    CH = N // QUARTERS
    JQ = CH // P
    JH = TILES // 2
    DIGITS = 4
    GROUP = P // DIGITS
    WORDS = GROUP // 2
    HALF = D + 1
    COLS = 2 * HALF
    XC = 512
    XT = XC // P
    CHUNKS = N // XC
    GJ = 8
    NG = TILES // GJ
    SLOPE = 0.2
    EPS = 1e-5
    LO = 2.0 ** 11
    TOP = 2.0 ** 25
    MASK = 0x4040
    NEG_BYTE = 47
    STEPS0 = 8

    adj_v = adj.rearrange("(t p) (q c) -> t p q c", p=P, q=QUARTERS)
    x_chunks = x.rearrange("(c k p) d -> c p k d", k=XT, p=P)
    XSLOTS = 4
    x_tiles = x.rearrange("(t p) d -> t p d", p=P)
    out_tiles = out.rearrange("(t p) d -> t p d", p=P)
    words_dram = nc.dram_tensor("words_dram", (TILES, P, TILES * WORDS), U16, kind="Internal").ap()
    xh_dram = nc.dram_tensor("xh_dram", (TILES, P, 2 * D), F32, kind="Internal").ap()

    def row(dram, t):
        return dram[ds(t, 1)].rearrange("o p d -> p (o d)")

    ctx = ExitStack()
    with ctx:
        def sb(name, shape, dtype):
            return ctx.enter_context(nc.sbuf_tensor(name, shape, dtype))

        def pb(name, shape, dtype):
            return ctx.enter_context(nc.psum_tensor(name, shape, dtype))

        def sem(name):
            return ctx.enter_context(nc.semaphore(name))

        s2_row = sb("s2_row", [P, N], F32)
        wts_pos = sb("wts_pos", [P, TILES, COLS], F16)
        wts_neg = sb("wts_neg", [P, TILES, COLS], F16)
        adj_in = sb("adj_in", [P, QUARTERS, CH], I32)
        h1_all = adj_in[:, :, :].rearrange("p q c -> p (q c)").bitcast(F32).rearrange("p (t d) -> p t d", d=D)
        present = sb("present", [P, QUARTERS, CH], U8)
        words_in = present[:, :, :].rearrange("p q c -> p (q c)").bitcast(U16).rearrange(
            "p (s w) -> p s w", w=TILES * WORDS)
        branch = sb("branch", [P, QUARTERS, CH], U8)
        words = sb("words", [P, 2, TILES, WORDS], U16)
        masks = sb("masks", [P, 2, 2, TILES, P], U8)
        xT_all = masks[:, :, :, :, :].rearrange("p a b t i -> p (a b t i)").bitcast(F32)
        h_all = wts_neg[:, :, :].rearrange("p t c -> p (t c)").bitcast(F32)[:, 0:TILES * D].rearrange(
            "p (t d) -> p t d", d=D)
        x_in = branch[:, :, :].rearrange("p q c -> p (q c)").bitcast(F32)[:, 0:XSLOTS * XT * D].rearrange(
            "p (b k d) -> p b k d", b=XSLOTS, k=XT) if N >= 8192 else sb("x_in", [P, XSLOTS, XT, D], F32)
        scratch = sb("scratch", [P, 2, GJ * D], F32)
        xT_sb = scratch[:, :, 0:XC]
        acc = sb("acc", [P, 2, 2 * COLS], F32)
        x_res = sb("x_res", [P, 2, D], F32)
        xh = sb("xh", [P, 2, 2 * D], F32)
        total = sb("total", [P, COLS], F32)
        num = sb("num", [P, HALF], F32)
        guarded = sb("guarded", [P, HALF], F32)
        pre = sb("pre", [P, 2, D], F32)
        w0_sb = sb("w0_sb", [P, D], F32)
        h_rhs = sb("h_rhs", [P, D + 2], F32)
        b0_row = sb("b0_row", [P, D], F32)
        w1_sb = sb("w1_sb", [P, D], F32)
        eye_sb = sb("eye_sb", [P, P], F32)
        rep = sb("rep", [P, P], F32)
        x1T_sb = rep
        ones = w0_sb
        b1_row = sb("b1_row", [P, D], F32)
        wdst_row = sb("wdst_row", [P, D], F32)
        mean_row = sb("mean_row", [P, HALF], F32)
        hsum = h_rhs[:, 0:D]
        packer_sb = sb("packer_sb", [P, WORDS], dt.bfloat16)
        a12_sb = sb("a12_sb", [P, 2], F32)
        b0_sb = sb("b0_sb", [P, 1], F32)
        dn = sb("dn", [P, 2, TILES, 2], F16)
        ba_sb = sb("ba_sb", [P, 1], F32)
        s12 = sb("s12", [P, TILES, 2], F32)
        s_dst = sb("s_dst", [P, TILES], F32)
        thr = sb("thr", [P, TILES], F32)
        zM = sb("zM", [P, TILES], F32)
        zlow = sb("zlow", [P, TILES], F32)
        alpha = sb("alpha", [P, TILES], F32)
        beta = sb("beta", [P, TILES], F32)
        v = sb("v", [P, 2, TILES], F32)
        vK = sb("vK", [P, 2, TILES], F32)
        vD = total[:, 0:2 * TILES].rearrange("p (k t) -> p k t", k=2)
        chunk_stats = sb("chunk_stats", [P, 2, CHUNKS], F32)
        hmax_t = sb("hmax_t", [P, TILES], F32)
        cst = sb("cst", [P, 10], F32)
        sig_bias = sb("sig_bias", [P, 1], F32)
        eps = sb("eps", [P, 1], F32)
        minus_half = sb("minus_half", [P, 1], F32)
        iszero = sb("iszero", [P, 1], F32)
        rden = sb("rden", [P, 2], F32)
        bn = sb("bn", [P, 6], F32)
        mv = sb("mv", [P, 2, 2], F32)
        veps = sb("veps", [P, 1], F32)
        rstd = sb("rstd", [P, 2], F32)

        psum = pb("psum", [P, 8, 512], F32)
        bank = [psum[:, i, :] for i in range(8)]
        acc_ps = [(bank[0], bank[1]), (bank[2], bank[3])]
        pack_ps = [bank[4], bank[5]]
        x1T_ps, h1_ps = bank[6], bank[7]
        xT_ps, s2_ps, small_ps = bank[0:2], bank[6:8], bank[7]

        def h_ps(b):
            return psum[:, 2 + 2 * b:4 + 2 * b, 0:2 * (D + 2)].rearrange("p n (k c) -> p n k c", c=D + 2)

        const_in = sem("const_in")
        dve_const = sem("dve_const")
        x_in_landed = [sem(f"x_in_landed{k}") for k in range(XSLOTS)]
        small_done, h_rhs_ready = sem("small_done"), sem("h_rhs_ready")
        xT_done, xT_copied, xT_kept = sem("xT_done"), sem("xT_copied"), sem("xT_kept")
        h_done, h_added, h_out = sem("h_done"), sem("h_added"), sem("h_out")
        s2_done, s2_copied = sem("s2_done"), sem("s2_copied")
        setup = sem("setup")
        hmax_in, hmax_out = sem("hmax_in"), sem("hmax_out")
        xsum_ready, hsum_done = sem("xsum_ready"), sem("hsum_done")
        exp_in, exp_out = sem("exp_in"), sem("exp_out")
        y_pos, y_neg = sem("y_pos"), sem("y_neg")
        hi_pos, hi_neg = sem("hi_pos"), sem("hi_neg")
        lo_pos, lo_neg = sem("lo_pos"), sem("lo_neg")
        den_step = sem("den_step")
        adj_landed = [sem(f"adj_landed{q}") for q in range(QUARTERS)]
        present_made, branch_made, edges_made = sem("present_made"), sem("branch_made"), sem("edges_made")
        packed, words_made = sem("packed"), sem("words_made")
        words_stored = [sem("words_stored0"), sem("words_stored1")]
        masks_made, acc_done, acc_copied = sem("masks_made"), sem("acc_done"), sem("acc_copied")
        x_res_landed = [sem("x_res_landed0"), sem("x_res_landed1")]
        fold, stats_made, veps_made, rstd_made = sem("fold"), sem("stats_made"), sem("veps_made"), sem("rstd_made")
        x1_made, x1T_done, x1T_copied, h1_done = sem("x1_made"), sem("x1T_done"), sem("x1T_copied"), sem("h1_done")
        h1_biased, h1_made, hsum_added = sem("h1_biased"), sem("h1_made"), sem("hsum_added")
        xh_stored = [sem("xh_stored0"), sem("xh_stored1")]
        h1_in = [sem(f"h1_in{g}") for g in range(NG)]
        max1_in, max1_out = sem("max1_in"), sem("max1_out")
        y1, hi1, lo1 = sem("y1"), sem("hi1"), sem("lo1")
        words_landed = [sem("words_landed0"), sem("words_landed1")]
        any_made, masks1_made, acc1_done, acc1_copied = sem("any_made"), sem("masks1_made"), sem("acc1_done"), sem("acc1_copied")
        x1_landed = [sem("x1_landed0"), sem("x1_landed1")]
        fold1, stats1, veps1, rstd1, out_made = sem("fold1"), sem("stats1"), sem("veps1"), sem("rstd1"), sem("out_made")
        out_stored = [sem("out_stored0"), sem("out_stored1")]

        act_passed, dve_passed, pe_passed = sem("act_passed"), sem("dve_passed"), sem("pe_passed")

        block = ctx.enter_context(nc.Block())
        CONSTS = 12

        @block.sync
        def _(sp):
            for k in range(XSLOTS):
                sp.dma_start(x_in[:, k], x_chunks[k]).then_inc(x_in_landed[k], 16)
            with sp.Fori(1, CHUNKS // XSLOTS) as u:
                for k in range(XSLOTS):
                    sp.wait_ge(xT_done, XSLOTS * u - XSLOTS + k + 1)
                    sp.dma_start(x_in[:, k], x_chunks[ds(XSLOTS * u + k, 1)].rearrange(
                        "o p k d -> p (o k) d")).then_inc(x_in_landed[k], 16)

            def feed(t):
                for q in range(QUARTERS):
                    sp.wait_ge(present_made, 4 * (t - 1) + q + 1)
                    sp.dma_start(adj_in[:, q, :], adj_v[ds(t, 1), :, q, :].rearrange(
                        "o p c -> p (o c)")).then_inc(adj_landed[q], 16)

            def residual(t, b, first=False):
                if not first:
                    sp.wait_ge(fold, STEPS0 * (t - 1))
                sp.dma_start(x_res[:, b, :], row(x_tiles, t)).then_inc(x_res_landed[b], 16)

            def store_words(t, b):
                sp.wait_ge(words_made, 2 * t + 2)
                sp.dma_start(row(words_dram, t), words[:, b].rearrange("p t w -> p (t w)")).then_inc(
                    words_stored[b], 16)

            def store_xh(t, b):
                sp.wait_ge(h1_made, t + 1)
                sp.dma_start(row(xh_dram, t), xh[:, b, :]).then_inc(xh_stored[b], 16)

            feed(1)
            feed(2)
            store_words(0, 0)
            for t in range(2):
                residual(t, t, first=True)
                feed(t + 3)
                store_words(t + 1, (t + 1) % 2)
            with sp.Fori(0, (TILES - 6) // 2) as u:
                for k in range(2):
                    t = 2 * u + k + 2
                    residual(t, k)
                    store_xh(t - 2, k)
                    feed(t + 3)
                    store_words(t + 1, 1 - k)
            for t in range(TILES - 4, TILES):
                residual(t, t % 2)
                store_xh(t - 2, t % 2)
                if t + 3 < TILES:
                    feed(t + 3)
                if t + 1 < TILES:
                    store_words(t + 1, (t + 1) % 2)
            sp.wait_ge(present_made, 4 * TILES)

            def load_h1(g):
                sp.dma_start(h1_all[:, GJ * g:GJ * (g + 1), :],
                             xh_dram[GJ * g:GJ * (g + 1), :, D:2 * D].rearrange("t p d -> p t d")).then_inc(
                    h1_in[g], 16)

            sp.wait_ge(xh_stored[0], 16 * (JH - 1))
            sp.wait_ge(xh_stored[1], 16 * (JH - 1))
            for g in range(NG - 1):
                load_h1(g)
            for b in range(2):
                sp.wait_ge(words_stored[b], 16 * JH)
            sp.wait_ge(edges_made, 4 * TILES)

            def load_words(t, b, first=False):
                if not first:
                    sp.wait_ge(any_made, t - 1)
                sp.dma_start(words_in[:, b, :], row(words_dram, t)).then_inc(words_landed[b], 16)

            def load_x1(t, b, first=False):
                if first:
                    sp.wait_ge(fold, STEPS0 * (TILES - 1 + b))
                else:
                    sp.wait_ge(fold1, 7 * (t - 1))
                sp.dma_start(x_res[:, b, :], xh_dram[ds(t, 1), :, 0:D].rearrange(
                    "o p d -> p (o d)")).then_inc(x1_landed[b], 16)

            def store_out(t, b):
                sp.wait_ge(out_made, t + 1)
                sp.dma_start(row(out_tiles, t), xh[:, b, 0:D]).then_inc(out_stored[b], 16)

            for t in range(2):
                load_words(t, t, first=True)
            for t in range(TILES - 2, TILES):
                store_xh(t, t % 2)
            for b in range(2):
                sp.wait_ge(xh_stored[b], 16 * JH)
            load_h1(NG - 1)
            for t in range(2):
                load_x1(t, t, first=True)
            for t in (0, 1):
                load_words(t + 2, t)
            with sp.Fori(0, (TILES - 4) // 2) as u:
                for b in range(2):
                    t = 2 * u + b + 2
                    load_words(t + 2, b)
                    load_x1(t, b)
                    store_out(t - 2, b)
            for t in range(TILES - 2, TILES):
                load_x1(t, t % 2)
                store_out(t - 2, t % 2)
            for t in range(TILES - 2, TILES):
                store_out(t, t % 2)
            for b in range(2):
                sp.wait_ge(out_stored[b], 16 * JH)

        @block.scalar
        def _(act):
            for dst, src in (
                (w0_sb[:, :], w0), (a12_sb[:, :], a12), (b0_sb[:, :], b0_col), (ba_sb[:, :], ba.to_broadcast([P, 1])),
                (h_rhs[:, 0:D], w0t), (eye_sb[:, :], eye), (b0_row[:, :], b0.to_broadcast([P, D])),
                (packer_sb[:, :], packer), (w1_sb[:, :], w1), (b1_row[:, :], b1.to_broadcast([P, D])),
                (wdst_row[:, :], watt[:, D:2 * D].to_broadcast([P, D])),
            ):
                act.dma_start(dst, src).then_inc(const_in, 16)

            def copy_xT(c, b, first=False):
                act.wait_ge(xT_done, c + 1)
                if not first:
                    act.wait_ge(h_done, c - 1)
                    act.wait_ge(xT_kept, c - 1)
                nc.scalar.activation(xT_sb[:, b, :], xT_ps[b], ACT.Identity,
                                     accum_out=chunk_stats[:, 1, ds(c, 1)]).then_inc(xT_copied, 1)

            for b in range(2):
                copy_xT(b, b, first=True)
            with act.Fori(1, CHUNKS // 4) as u:
                for b in range(2):
                    copy_xT(2 * u + b, b)
            for q in range(QUARTERS):
                act.dma_start(adj_in[:, q, :], adj_v[0, :, q, :]).then_inc(adj_landed[q], 16)
            with act.Fori(CHUNKS // 4, CHUNKS // 2) as u:
                for b in range(2):
                    copy_xT(2 * u + b, b)

            def copy_s2(first, last):
                with act.Fori(first // 2, last // 2) as u:
                    for b in range(2):
                        act.wait_ge(s2_done, 2 * u + b + 1)
                        nc.scalar.copy(s2_row[:, ds((2 * u + b) * XC, XC)], s2_ps[b]).then_inc(s2_copied, 1)

            copy_s2(0, CHUNKS // 4)
            act.wait_ge(exp_in, 1)
            nc.scalar.activation(v[:, 0, :], s12[:, :, 1], ACT.Exp, bias=cst[:, 3:4])
            nc.scalar.activation(v[:, 1, :], s12[:, :, 1], ACT.Exp, bias=cst[:, 4:5], scale=SLOPE)
            nc.scalar.activation(alpha[:, :], zM[:, :], ACT.Exp)
            nc.scalar.activation(beta[:, :], zlow[:, :], ACT.Exp).then_inc(exp_out, 1)

            def make_present(t, q, nth):
                act.wait_ge(adj_landed[q], 16 * t + 16)
                if nth:
                    act.wait_ge(edges_made, 4 * t - 4 + q + 1)
                act.sem_inc(act_passed, 1)
                nc.scalar.activation(present[:, q, :].bitcast(F8), adj_in[:, q, :], ACT.Sigmoid,
                                     bias=sig_bias[:, 0:1], scale=64.0, saturate=False).then_inc(present_made, 1)

            def copy_words(t, b, half, free=None):
                act.wait_ge(packed, 4 * t + 2 * half + 2)
                if free is not None:
                    act.wait_ge(masks_made, t - 1)
                    act.wait_ge(words_stored[b], 16 * free)
                nc.scalar.copy(words[:, b, half * JH:(half + 1) * JH, :],
                               pack_ps[half][:, 0:JH * WORDS].rearrange("p (j w) -> p j w", w=WORDS)).then_inc(
                    words_made, 1)

            def copy_acc(t, b, older=True):
                act.wait_ge(acc_done, t + 1)
                if older:
                    act.wait_ge(fold, STEPS0 * (t - 2) + 1 if not isinstance(t, int) or t > 1 else 1)
                nc.scalar.mul(acc[:, b, 0:COLS], acc_ps[b][0][:, 0:COLS], alpha[:, ds(t, 1)])
                nc.scalar.mul(acc[:, b, COLS:2 * COLS], acc_ps[b][1][:, 0:COLS], beta[:, ds(t, 1)]).then_inc(
                    acc_copied, 1)

            def copy_x1T(t):
                act.wait_ge(x1T_done, t + 1)
                nc.scalar.copy(x1T_sb[:, :], x1T_ps[:, 0:P]).then_inc(x1T_copied, 1)

            def hi_halves(n):
                g = NG - 1 - n
                for made, kind, wts, done in ((y_pos, 0, wts_pos, hi_pos), (y_neg, 1, wts_neg, hi_neg)):
                    act.wait_ge(made, n + 1)
                    nc.scalar.mul(wts[:, GJ * g:GJ * (g + 1), 0:D],
                                  scratch[:, kind, :].rearrange("p (j d) -> p j d", d=D), 1.0 / LO).then_inc(done, 1)

            def quarters(n):
                return range(QUARTERS * n // early, QUARTERS * (n + 1) // early)

            early = NG // 2
            for q in quarters(0):
                make_present(0, q, 0)
            for n in range(early):
                for q in quarters(n):
                    if q + 1 < QUARTERS:
                        copy_s2((q + 1) * CHUNKS // 4, (q + 2) * CHUNKS // 4)
                hi_halves(n)
                if n + 1 < early:
                    for q in quarters(n + 1):
                        make_present(0, q, 0)
            copy_words(0, 0, 0)
            copy_words(0, 0, 1)
            for n in range(early):
                hi_halves(early + n)
                for q in quarters(n):
                    make_present(1, q, 1)
            make_present(2, 0, 1)
            copy_words(1, 1, 0)
            make_present(2, 1, 1)
            copy_words(1, 1, 1)
            make_present(2, 2, 1)
            make_present(2, 3, 1)

            def iteration(t, b, free, last=False, older=True):
                copy_acc(t - 1, 1 - b, older)
                if not last:
                    make_present(t + 2, 0, 1)
                copy_words(t + 1, 1 - b, 0, free)
                if not last:
                    make_present(t + 2, 1, 1)
                copy_words(t + 1, 1 - b, 1, free)
                copy_x1T(t - 1)
                if not last:
                    make_present(t + 2, 2, 1)
                    make_present(t + 2, 3, 1)

            iteration(1, 1, 1, older=False)
            iteration(2, 0, 1, older=False)
            with act.Fori(0, (TILES - 6) // 2) as u:
                for k in range(2):
                    t = 2 * u + k + 3
                    iteration(t, 1 - k, u + 2)
            iteration(TILES - 3, 1, JH - 1)
            iteration(TILES - 2, 0, JH - 1, last=True)
            copy_acc(TILES - 2, 0)
            copy_x1T(TILES - 2)
            copy_acc(TILES - 1, 1)
            copy_x1T(TILES - 1)

            act.wait_ge(max1_out, 3)
            nc.scalar.activation(v[:, 0, :], s_dst[:, :], ACT.Exp, bias=cst[:, 3:4]).then_inc(exp_out, 1)
            for g in range(NG):
                act.wait_ge(y1, g + 1)
                nc.scalar.mul(wts_pos[:, GJ * g:GJ * (g + 1), 0:D],
                              scratch[:, g % 2, :].rearrange("p (j d) -> p j d", d=D), 1.0 / LO).then_inc(hi1, 1)

            def copy_acc1(t, b, older=True):
                act.wait_ge(acc1_done, t + 1)
                if older:
                    act.wait_ge(fold1, 7 * (t - 2) + 1)
                nc.scalar.copy(acc[:, b, 0:COLS], acc_ps[b][0][:, 0:COLS]).then_inc(acc1_copied, 1)

            copy_acc1(0, 0, older=False)
            copy_acc1(1, 1, older=False)
            with act.Fori(1, JH) as u:
                for b in range(2):
                    copy_acc1(2 * u + b, b)

        @block.vector
        def _(dve):
            nc.vector.memset(sig_bias[:, :], -32.0)
            nc.vector.memset(minus_half[:, :], -0.5)
            nc.vector.memset(eps[:, :], EPS)
            dve.wait_ge(const_in, 16 * (CONSTS - 1))
            nc.vector.tensor_copy(rep[:, :], b0_sb[:, 0:1].to_broadcast([P, P])).then_inc(dve_const, 1)
            dve.wait_ge(small_done, 1)
            nc.vector.tensor_copy(h_rhs[:, D:D + 2], small_ps[:, 0:2])
            nc.vector.tensor_copy(rep[:, :], small_ps[:, 1:2].to_broadcast([P, P]))
            nc.vector.memset(ones[:, :], 1.0)
            nc.vector.tensor_tensor(cst[:, 8:9], small_ps[:, 2:3], ba_sb[:, 0:1], ALU.add).then_inc(h_rhs_ready, 1)
            dve.wait_ge(h_rhs_ready, 1)
            nc.vector.tensor_tensor(cst[:, 9:10], small_ps[:, 3:4], cst[:, 8:9], ALU.add).then_inc(h_rhs_ready, 1)

            with dve.Fori(0, CHUNKS // 4) as u:
                for k in range(4):
                    c = 4 * u + k
                    dve.wait_ge(h_done, c + 1)
                    nc.vector.tensor_copy(
                        s12[:, ds(c * XT, XT), :].rearrange("p (n k) c -> p n k c", n=2), h_ps(k % 2)[:, :, :, D:D + 2])
                    nc.vector.tensor_tensor(
                        h_all[:, ds(c * XT, XT), :].rearrange("p (n k) d -> p n k d", n=2), h_ps(k % 2)[:, :, :, 0:D],
                        b0_row[:, :].unsqueeze(1).unsqueeze(1).to_broadcast([P, 2, 2, D]), ALU.add).then_inc(h_out, 1)
                dve.wait_ge(h_out, 4 * u + 4)
                nc.vector.tensor_reduce(chunk_stats[:, 0, ds(u, 1)],
                                        h_all[:, ds(u * 4 * XT, 4 * XT), :].rearrange("p k d -> p (k d)"), AX.X, ALU.max,
                                        apply_absolute_value=True).then_inc(h_added, 1)

            steps = [0]

            def step(ins):
                steps[0] += 1
                ins.then_inc(setup, 1)
                dve.wait_ge(setup, steps[0])

            dve.wait_ge(h_added, CHUNKS // 4)
            nc.vector.tensor_reduce(cst[:, 1:2], chunk_stats[:, 0, 0:CHUNKS // 4], AX.X, ALU.max)
            nc.vector.tensor_reduce(cst[:, 0:1], s12[:, :, 1], AX.X, ALU.max).then_inc(hmax_in, 1)
            nc.vector.tensor_scalar(thr[:, :], s12[:, :, 0], cst[:, 9:10], -1.0, ALU.add, ALU.mult)
            dve.wait_ge(xT_copied, CHUNKS)
            step(nc.vector.tensor_reduce(cst[:, 2:3], chunk_stats[:, 1, :], AX.X, ALU.add))
            dve.wait_ge(hmax_out, 1)
            nc.vector.tensor_scalar(cst[:, 3:4], cst[:, 0:1], -1.0, None, ALU.mult)
            nc.vector.tensor_scalar(cst[:, 4:5], cst[:, 0:1], -SLOPE, None, ALU.mult)
            step(nc.vector.tensor_scalar(zM[:, :], s12[:, :, 0], cst[:, 9:10], cst[:, 0:1], ALU.add, ALU.add))
            step(nc.vector.scalar_tensor_tensor(zlow[:, :], zM[:, :], SLOPE, zM[:, :], ALU.mult, ALU.max))
            step(nc.vector.tensor_tensor(alpha[:, :], zM[:, :], zlow[:, :], ALU.subtract))
            step(nc.vector.scalar_tensor_tensor(zlow[:, :], zM[:, :], SLOPE, zlow[:, :], ALU.mult, ALU.subtract))
            nc.vector.tensor_copy(zM[:, :], alpha[:, :]).then_inc(exp_in, 1)

            def scales(layer_done):
                step(nc.vector.tensor_scalar(cst[:, 5:6], cst[:, 1:2], 1e-30, None, ALU.max))
                step(nc.vector.tensor_scalar(cst[:, 5:6].bitcast(I32), cst[:, 5:6].bitcast(I32), 0x7F800000,
                                             None, ALU.bitwise_and))
                step(nc.vector.reciprocal(cst[:, 6:7], cst[:, 5:6]))
                nc.vector.tensor_scalar(cst[:, 8:9], cst[:, 6:7], 1.0 / N, None, ALU.mult)
                step(nc.vector.tensor_scalar(cst[:, 7:8], cst[:, 6:7], TOP, None, ALU.mult))

            def denominators(kinds):
                for kind in kinds:
                    nc.vector.tensor_scalar(vK[:, kind, :], v[:, kind, :], cst[:, 7:8], None, ALU.mult)
                    nc.vector.tensor_scalar(vD[:, kind, :], v[:, kind, :], TOP, None, ALU.mult).then_inc(den_step, 1)
                dve.wait_ge(den_step, den_steps[0] + len(kinds))
                for kind in kinds:
                    nc.vector.tensor_scalar(dn[:, kind, :, 0], vD[:, kind, :], 1.0 / LO, None, ALU.mult).then_inc(den_step, 1)
                dve.wait_ge(den_step, den_steps[0] + 2 * len(kinds))
                for kind in kinds:
                    nc.vector.scalar_tensor_tensor(dn[:, kind, :, 1], dn[:, kind, :, 0], -LO, vD[:, kind, :],
                                                   ALU.mult, ALU.add).then_inc(den_step, 1)
                den_steps[0] += 3 * len(kinds)
                dve.wait_ge(den_step, den_steps[0])

            den_steps = [0]
            scales(0)
            dve.wait_ge(exp_out, 1)
            denominators((0, 1))

            def product(kind, vkind, g, src):
                return nc.vector.tensor_tensor(
                    scratch[:, kind, :].rearrange("p (j d) -> p j d", d=D), src[:, GJ * g:GJ * (g + 1), :],
                    vK[:, vkind, GJ * g:GJ * (g + 1)].unsqueeze(2).to_broadcast([P, GJ, D]), ALU.mult)

            def low_half(wts, kind, dkind, g):
                nc.vector.tensor_copy(wts[:, GJ * g:GJ * (g + 1), :].rearrange("p j (s c) -> p j s c", s=2)[:, :, :, D],
                                      dn[:, dkind, GJ * g:GJ * (g + 1), :])
                return nc.vector.scalar_tensor_tensor(
                    wts[:, GJ * g:GJ * (g + 1), HALF:HALF + D], wts[:, GJ * g:GJ * (g + 1), 0:D], -LO,
                    scratch[:, kind, :].rearrange("p (j d) -> p j d", d=D), ALU.mult, ALU.add)

            def make_branch(t, q, older=True):
                if older:
                    dve.wait_ge(packed, 4 * t - 4 + q + 1)
                nc.vector.tensor_scalar(branch[:, q, :], s2_row[:, q * CH:(q + 1) * CH],
                                        thr[:, ds(t, 1)], NEG_BYTE, ALU.is_gt, ALU.add).then_inc(
                    branch_made, 1)

            def make_s2_wait(tile, q):
                if tile == 0:
                    dve.wait_ge(s2_copied, (q + 1) * CHUNKS // 4)

            def make_edges(t, q):
                dve.wait_ge(branch_made, 4 * t + q + 1)
                dve.wait_ge(present_made, 4 * t + q + 1)
                nc.vector.tensor_tensor(branch[:, q, :].bitcast(U16), branch[:, q, :].bitcast(U16),
                                        present[:, q, :].bitcast(U16), ALU.bitwise_and).then_inc(edges_made, 1)

            def pieces(t):
                make_branch(t, 0)
                for q in range(1, QUARTERS):
                    make_branch(t, q)
                    make_edges(t, q - 1)
                make_edges(t, QUARTERS - 1)

            def unpack(src, dst, odd):
                to = dst.bitcast(U16)
                for k in range(DIGITS):
                    left = 6 - 2 * k - odd
                    last = nc.vector.tensor_scalar(
                        to[:, :, WORDS * k:WORDS * (k + 1)], src, abs(left), MASK,
                        ALU.logical_shift_left if left >= 0 else ALU.logical_shift_right, ALU.bitwise_and)
                return last

            def make_masks(t, b, older=True):
                dve.wait_ge(words_made, 2 * t + 2)
                if older:
                    dve.wait_ge(acc_done, t - 1)
                unpack(words[:, b], masks[:, b, 1], 0)
                unpack(words[:, b], masks[:, b, 0], 1).then_inc(masks_made, 1)

            def fold_tile(done, t, b, two_branches, copied, landed, nth, stats):
                n = [0]
                count = STEPS0 if two_branches else STEPS0 - 1

                def chained(ins):
                    n[0] += 1
                    ins.then_inc(done, 1)
                    dve.wait_ge(done, count * t + n[0])

                dve.wait_ge(copied, t + 1)
                src = acc[:, b, 0:COLS]
                if two_branches:
                    chained(nc.vector.tensor_tensor(total[:, :], acc[:, b, 0:COLS], acc[:, b, COLS:2 * COLS], ALU.add))
                    src = total[:, :]
                chained(nc.vector.scalar_tensor_tensor(num[:, :], src[:, HALF:COLS], 1.0 / LO, src[:, 0:HALF],
                                                       ALU.mult, ALU.add))
                chained(nc.vector.tensor_scalar(iszero[:, :], num[:, D:HALF], 0.0, None, ALU.is_equal))
                chained(nc.vector.scalar_tensor_tensor(guarded[:, :], mean_row[:, :], iszero[:, 0:1], num[:, :],
                                                       ALU.mult, ALU.add))
                chained(nc.vector.reciprocal(rden[:, 0:1], guarded[:, D:HALF]))
                chained(nc.vector.tensor_scalar(rden[:, 1:2], rden[:, 0:1], cst[:, 5:6], None, ALU.mult))
                dve.wait_ge(landed, nth)
                chained(nc.vector.scalar_tensor_tensor(pre[:, b, :], guarded[:, 0:D], rden[:, 1:2], x_res[:, b, :],
                                                       ALU.mult, ALU.add))
                chained(nc.vector.bn_stats(bn[:, :], pre[:, b, :]))
                dve.sem_inc(dve_passed, 1)
                nc.vector.bn_aggr(mv[:, b, :], bn[:, :]).then_inc(stats, 1)

            def normalise(t, b, ready, made, stored, nth):
                dve.wait_ge(ready, t + 1)
                if nth is not None:
                    dve.wait_ge(stored, nth)
                nc.vector.tensor_scalar(xh[:, b, 0:D], pre[:, b, :], mv[:, b, 0:1], rstd[:, b:b + 1],
                                        ALU.subtract, ALU.mult).then_inc(made, 1)

            def finish_h1(t, b, older=True):
                dve.wait_ge(h1_done, t + 1)
                if older:
                    dve.wait_ge(hsum_added, t)
                nc.vector.tensor_tensor(xh[:, b, D:2 * D], h1_ps[:, 0:D], b1_row[:, :], ALU.add).then_inc(h1_biased, 1)
                dve.wait_ge(h1_biased, t + 1)
                nc.vector.scalar_tensor_tensor(num[:, 0:D], xh[:, b, D:2 * D], 1.0, wdst_row[:, :], ALU.mult,
                                               ALU.mult, accum_out=s_dst[:, ds(t, 1)])
                nc.vector.tensor_reduce(hmax_t[:, ds(t, 1)], xh[:, b, D:2 * D], AX.X, ALU.max,
                                        apply_absolute_value=True).then_inc(h1_made, 1)

            early = NG // 2
            for n in range(NG):
                g = NG - 1 - n
                if n >= 1:
                    dve.wait_ge(lo_pos, n)
                product(0, 0, g, h_all).then_inc(y_pos, 1)
                if n == early:
                    nc.vector.tensor_scalar(rep[:, :], ones[:, :], cst[:, 2:3], None, ALU.mult).then_inc(xsum_ready, 1)
                    make_masks(0, 0, older=False)
                tile, first = divmod(n, early)
                for q in range(QUARTERS * first // early, QUARTERS * (first + 1) // early):
                    make_s2_wait(tile, q)
                    make_branch(tile, q, older=bool(tile))
                    make_edges(tile, q)
                for kind, wts, hi, made, lo in ((0, wts_pos, hi_pos, y_pos, lo_pos), (1, wts_neg, hi_neg, y_neg, lo_neg)):
                    dve.wait_ge(made, n + 1)
                    dve.wait_ge(hi, n + 1)
                    low_half(wts, kind, kind, g).then_inc(lo, 1)
            dve.wait_ge(hsum_done, 1)
            nc.vector.memset(mean_row[:, D:HALF], 1.0)
            step(nc.vector.scalar_tensor_tensor(mean_row[:, 0:D], small_ps[:, 0:D], 1.0 / N, b0_row[:, :],
                                                ALU.mult, ALU.add))
            step(nc.vector.tensor_scalar(mean_row[:, 0:D], mean_row[:, 0:D], cst[:, 6:7], None, ALU.mult))
            make_masks(1, 1, older=False)

            def iteration(t, b, nth, last=False):
                if not last:
                    pieces(t + 1)
                fold_tile(fold, t - 1, 1 - b, True, acc_copied, x_res_landed[1 - b], 16 * nth, stats_made)
                if not isinstance(t, int) or t >= 2:
                    finish_h1(t - 2, b, older=not isinstance(t, int) or t >= 3)
                normalise(t - 1, 1 - b, rstd_made, x1_made, xh_stored[1 - b],
                          None if isinstance(t, int) and t < 3 else 16 * (nth - 1))
                if not last:
                    make_masks(t + 1, 1 - b)

            for t in (1, 2):
                iteration(t, t % 2, (t - 1) // 2 + 1)
            with dve.Fori(0, (TILES - 4) // 2) as u:
                for k in range(2):
                    iteration(2 * u + k + 3, 1 - k, u + 2)
            iteration(TILES - 1, 1, JH, last=True)
            fold_tile(fold, TILES - 1, 1, True, acc_copied, x_res_landed[1], 16 * JH, stats_made)
            finish_h1(TILES - 2, 0)
            normalise(TILES - 1, 1, rstd_made, x1_made, xh_stored[1], 16 * (JH - 1))
            finish_h1(TILES - 1, 1)

            dve.wait_ge(h1_made, TILES)
            nc.vector.tensor_reduce(cst[:, 0:1], s_dst[:, :], AX.X, ALU.max)
            nc.vector.tensor_reduce(cst[:, 1:2], hmax_t[:, :], AX.X, ALU.max).then_inc(max1_in, 1)
            dve.wait_ge(max1_out, 1)
            nc.vector.tensor_scalar(cst[:, 3:4], cst[:, 0:1], -1.0, None, ALU.mult).then_inc(max1_out, 2)
            scales(1)
            dve.wait_ge(exp_out, 2)
            denominators((0,))
            dve.wait_ge(acc_done, TILES)

            def make_masks1(t, b, older=True, nth=None):
                dve.wait_ge(words_landed[b], nth)
                flat = words[:, b].rearrange("p t w -> p (t w)")
                nc.vector.scalar_tensor_tensor(flat, words_in[:, b, :], 1, words_in[:, b, :],
                                               ALU.logical_shift_right, ALU.bitwise_or).then_inc(any_made, 1)
                dve.wait_ge(any_made, t + 1)
                if older:
                    dve.wait_ge(acc1_done, t - 1)
                unpack(words[:, b], masks[:, b, 0], 0).then_inc(masks1_made, 1)

            make_masks1(0, 0, older=False, nth=16)
            for g in range(NG):
                dve.wait_ge(h1_in[g], 16)
                if g >= 2:
                    dve.wait_ge(lo1, g - 1)
                product(g % 2, 0, g, h1_all).then_inc(y1, 1)
                if g >= 1:
                    dve.wait_ge(hi1, g)
                    low_half(wts_pos, (g - 1) % 2, 0, g - 1).then_inc(lo1, 1)
            dve.wait_ge(hi1, NG)
            low_half(wts_pos, (NG - 1) % 2, 0, NG - 1).then_inc(lo1, 1)
            dve.wait_ge(hsum_done, 2)
            nc.vector.tensor_scalar(mean_row[:, 0:D], h1_ps[:, 0:D], cst[:, 8:9], None, ALU.mult)
            make_masks1(1, 1, older=False, nth=16)

            def iteration1(t, b, nth, nth_w, last=False, older=True):
                if not last:
                    make_masks1(t + 1, 1 - b, nth=nth_w)
                fold_tile(fold1, t - 1, 1 - b, False, acc1_copied, x1_landed[1 - b], 16 * nth, stats1)
                normalise(t - 1, 1 - b, rstd1, out_made, out_stored[1 - b], 16 * (nth - 1) if older else None)

            iteration1(1, 1, 1, 32, older=False)
            iteration1(2, 0, 1, 32, older=False)
            with dve.Fori(0, (TILES - 4) // 2) as u:
                for k in range(2):
                    iteration1(2 * u + k + 3, 1 - k, u + 2, 16 * u + 48)
            iteration1(TILES - 1, 1, JH, None, last=True)
            iteration1(TILES, 0, JH, None, last=True)

        @block.gpsimd
        def _(pool):
            def keep_xT(c, b):
                pool.wait_ge(xT_copied, c + 1)
                nc.gpsimd.tensor_copy(xT_all[:, ds(c * XC, XC)], xT_sb[:, b, :]).then_inc(xT_kept, 1)

            with pool.Fori(0, CHUNKS // 2) as u:
                for b in range(2):
                    keep_xT(2 * u + b, b)
            pool.wait_ge(hmax_in, 1)
            nc.gpsimd.partition_all_reduce(cst[:, 0:2], cst[:, 0:2], P, MAX).then_inc(hmax_out, 1)
            pool.wait_ge(den_step, 6)
            for n in range(NG):
                g = NG - 1 - n
                if n >= 1:
                    pool.wait_ge(lo_neg, n)
                nc.gpsimd.tensor_tensor(
                    scratch[:, 1, :].rearrange("p (j d) -> p j d", d=D), h_all[:, GJ * g:GJ * (g + 1), :],
                    vK[:, 1, GJ * g:GJ * (g + 1)].unsqueeze(2).to_broadcast([P, GJ, D]), ALU.mult).then_inc(y_neg, 1)

            def inverse_std(t, b, made, veps_s, done):
                pool.wait_ge(made, t + 1)
                nc.gpsimd.tensor_tensor(veps[:, :], mv[:, b, 1:2], eps[:, :], ALU.add).then_inc(veps_s, 1)
                pool.wait_ge(veps_s, t + 1)
                nc.gpsimd.tensor_tensor(rstd[:, b:b + 1], veps[:, :], minus_half[:, :], ALU.pow).then_inc(done, 1)

            def add_h(t, b):
                pool.wait_ge(h1_made, t + 1)
                nc.gpsimd.tensor_tensor(hsum[:, :], hsum[:, :], xh[:, b, D:2 * D], ALU.add).then_inc(hsum_added, 1)

            pool.wait_ge(hsum_done, 1)
            nc.gpsimd.memset(hsum[:, :], 0.0)
            inverse_std(0, 0, stats_made, veps_made, rstd_made)
            with pool.Fori(0, (TILES - 2) // 2) as u:
                for k in range(2):
                    t = 2 * u + k + 1
                    inverse_std(t, 1 - k, stats_made, veps_made, rstd_made)
                    add_h(t - 1, k)
            inverse_std(TILES - 1, 1, stats_made, veps_made, rstd_made)
            add_h(TILES - 2, 0)
            add_h(TILES - 1, 1)
            pool.wait_ge(max1_in, 1)
            nc.gpsimd.partition_all_reduce(cst[:, 0:2], cst[:, 0:2], P, MAX).then_inc(max1_out, 1)
            with pool.Fori(0, JH) as u:
                for b in range(2):
                    inverse_std(2 * u + b, b, stats1, veps1, rstd1)

        @block.tensor
        def _(pe):
            pe.wait_ge(const_in, 16 * (CONSTS - 1))
            pe.wait_ge(dve_const, 1)
            nc.tensor.matmul(small_ps[:, 0:2], w0_sb[:, :], a12_sb[:, :], start=True, stop=True)
            nc.tensor.matmul(small_ps[:, 2:4], rep[:, :], a12_sb[:, :], start=True, stop=True).then_inc(small_done, 1)

            def transpose_x(c, k, nth, older=True):
                pe.wait_ge(x_in_landed[k], nth)
                if older:
                    pe.wait_ge(xT_copied, c - 1)
                for i in range(XT):
                    last = nc.tensor.transpose(xT_ps[k % 2][:, i * P:(i + 1) * P], x_in[:, k, i, :], eye_sb[:, :])
                last.then_inc(xT_done, 1)

            def make_h(c, b, older=True):
                pe.wait_ge(xT_copied, c + 1)
                if older:
                    pe.wait_ge(h_out, c - 1)
                for i in range(XT):
                    last = nc.tensor.matmul(h_ps(b)[:, i // 2, i % 2, :], xT_sb[:, b, i * P:(i + 1) * P], h_rhs[:, :],
                                            start=True, stop=True)
                last.then_inc(h_done, 1)

            pe.wait_ge(h_rhs_ready, 2)
            for c in range(XSLOTS):
                transpose_x(c, c, 16, older=c >= 2)
                if c:
                    make_h(c - 1, (c - 1) % 2, older=c >= 3)
            with pe.Fori(1, CHUNKS // XSLOTS) as u:
                for k in range(XSLOTS):
                    transpose_x(XSLOTS * u + k, k, 16 * u + 16)
                    make_h(XSLOTS * u + k - 1, (k + 1) % 2)
            make_h(CHUNKS - 1, 1)
            for c in range(2):
                pe.wait_ge(xT_kept, c + 1)
                nc.tensor.matmul(s2_ps[c], rep[:, :], xT_all[:, c * XC:(c + 1) * XC], start=True, stop=True).then_inc(
                    s2_done, 1)
            with pe.Fori(1, CHUNKS // 2) as u:
                for b in range(2):
                    pe.wait_ge(xT_kept, 2 * u + b + 1)
                    pe.wait_ge(s2_copied, 2 * u + b - 1)
                    nc.tensor.matmul(s2_ps[b], rep[:, :], xT_all[:, ds((2 * u + b) * XC, XC)], start=True,
                                     stop=True).then_inc(s2_done, 1)
            def pack(t, q, older=True):
                pe.wait_ge(edges_made, 4 * t + q + 1)
                if older:
                    pe.wait_ge(words_made, 2 * t - 2 + q // 2 + 1)
                pe.sem_inc(pe_passed, 1)
                for j in range(JQ * q, JQ * (q + 1)):
                    at = WORDS * (j % JH)
                    last = nc.tensor.matmul(pack_ps[j // JH][:, at:at + WORDS],
                                            branch[:, q, P * (j % JQ):P * (j % JQ) + P].bitcast(F8),
                                            packer_sb[:, :], start=True, stop=True)
                last.then_inc(packed, 1)

            def multiply(t, b, jobs=(), older=True, weights=False):
                pe.wait_ge(masks_made, t + 1)
                if older:
                    pe.wait_ge(acc_copied, t - 1)
                pe.sem_inc(pe_passed, 1)
                for j in range(TILES):
                    if weights and j % GJ == 0:
                        pe.wait_ge(lo_pos, j // GJ + 1)
                        pe.wait_ge(lo_neg, j // GJ + 1)
                    n, j = j, TILES - 1 - j
                    for kind, wts in ((1, wts_neg), (0, wts_pos)):
                        last = nc.tensor.matmul(acc_ps[b][kind][:, 0:COLS], masks[:, b, kind, j, :].bitcast(F8),
                                                wts[:, j, :], start=(n == 0), stop=(n == TILES - 1))
                    for at, job in jobs:
                        if n == at * TILES // 64:
                            job()
                last.then_inc(acc_done, 1)

            def transpose_x1(t, b):
                pe.wait_ge(x1_made, t + 1)
                nc.tensor.transpose(x1T_ps[:, 0:P], xh[:, b, 0:D], eye_sb[:, :]).then_inc(x1T_done, 1)

            def make_h1(t, older=True):
                pe.wait_ge(x1T_copied, t + 1)
                if older:
                    pe.wait_ge(h1_made, t)
                nc.tensor.matmul(h1_ps[:, 0:D], x1T_sb[:, :], w1_sb[:, :], start=True, stop=True).then_inc(h1_done, 1)

            def iteration(t, b, older=True, last=False, older_h=True):
                jobs = [(48, lambda: transpose_x1(t - 1, 1 - b)), (60, lambda: make_h1(t - 1, older_h))]
                if not last:
                    jobs += [(8 * (q + 1) + 2, lambda q=q: pack(t + 1, q)) for q in range(QUARTERS)]
                multiply(t, b, jobs, older)

            for q in range(QUARTERS):
                pack(0, q, older=False)
            pe.wait_ge(s2_copied, CHUNKS)
            pe.wait_ge(xsum_ready, 1)
            nc.tensor.matmul(small_ps[:, 0:D], rep[:, :], h_rhs[:, 0:D], start=True, stop=True).then_inc(hsum_done, 1)
            multiply(0, 0, [(32 + 8 * (q + 1) - 2, lambda q=q: pack(1, q)) for q in range(QUARTERS)], older=False,
                     weights=True)
            iteration(1, 1, older=False, older_h=False)
            iteration(2, 0)
            with pe.Fori(0, (TILES - 4) // 2) as u:
                for k in range(2):
                    iteration(2 * u + k + 3, 1 - k)
            iteration(TILES - 1, 1, last=True)
            transpose_x1(TILES - 1, 1)
            make_h1(TILES - 1)

            pe.wait_ge(hsum_added, TILES)
            pe.wait_ge(h1_made, TILES)
            nc.tensor.matmul(h1_ps[:, 0:D], ones[:, :], hsum[:, :], start=True, stop=True).then_inc(hsum_done, 1)

            def multiply1(t, b, older=True, weights=False):
                pe.wait_ge(masks1_made, t + 1)
                if older:
                    pe.wait_ge(acc1_copied, t - 1)
                pe.sem_inc(pe_passed, 1)
                for j in range(TILES):
                    if weights and j % GJ == 0:
                        pe.wait_ge(lo1, j // GJ + 1)
                    last = nc.tensor.matmul(acc_ps[b][0][:, 0:COLS], masks[:, b, 0, j, :].bitcast(F8),
                                            wts_pos[:, j, :], start=(j == 0), stop=(j == TILES - 1))
                last.then_inc(acc1_done, 1)

            multiply1(0, 0, older=False, weights=True)
            multiply1(1, 1, older=False)
            with pe.Fori(1, JH) as u:
                for b in range(2):
                    multiply1(2 * u + b, b)


def kernel(x, adj, L0_gnn_W, L0_gnn_b_W, L0_gnn_a_vec, L0_gnn_b_a, L1_gnn_W_fc, L1_gnn_b_fc, L1_gnn_w_att,
           L1_gnn_b_att):
    import ml_dtypes
    import numpy as np
    import concourse.bacc as bacc
    from concourse import mybir
    from concourse.bass_utils import run_bass_kernel_spmd

    i = np.arange(128)
    place = 4.0 * 4.0 ** (i // 32) * 256.0 ** (i % 2)
    packer = np.where((i % 32 // 2)[:, None] == np.arange(16)[None, :], place[:, None], 0.0).astype(ml_dtypes.bfloat16)
    arrays = {
        "x": x, "adj": adj, "w0": L0_gnn_W, "w0t": np.asarray(L0_gnn_W).T, "b0_col": np.reshape(L0_gnn_b_W, (-1, 1)),
        "b0": np.reshape(L0_gnn_b_W, (1, -1)),
        "a12": np.reshape(L0_gnn_a_vec, (2, -1)).T, "ba": np.reshape(L0_gnn_b_a, (1, 1)),
        "w1": L1_gnn_W_fc, "b1": np.reshape(L1_gnn_b_fc, (1, -1)), "watt": np.reshape(L1_gnn_w_att, (1, -1)),
        "packer": packer, "eye": np.eye(128, dtype=np.float32),
    }
    arrays = {f"in_{name}": np.ascontiguousarray(a) for name, a in arrays.items()}
    nc = bacc.Bacc("TRN2", target_bir_lowering=False, num_devices=1)
    ins = [nc.dram_tensor(name, a.shape, mybir.dt.from_np(a.dtype), kind="ExternalInput").ap()
           for name, a in arrays.items()]
    out = nc.dram_tensor("out", x.shape, mybir.dt.float32, kind="ExternalOutput").ap()
    build_two_layer_gat(nc, *ins, out)
    return run_bass_kernel_spmd(nc, [arrays], core_ids=[0]).results[0]["out"]
```

```python
def build_two_layer_gat(nc, x, adj, w0, w0t, b0_col, b0, a12, ba, w1, b1, watt, packer, eye, out):
    import concourse.bass as bass
    from concourse import mybir
    from contextlib import ExitStack

    dt = mybir.dt
    F32, F16, F8 = dt.float32, dt.float16, dt.float8e4
    U8, U16, U32, I32 = dt.uint8, dt.uint16, dt.uint32, dt.int32
    ALU, ACT, AX = mybir.AluOpType, mybir.ActivationFunctionType, mybir.AxisListType
    MAX = bass.bass_isa.ReduceOp.max
    ds = bass.ds

    P = 128
    N, D = x.shape
    TILES = N // P
    QUARTERS = 4
    CH = N // QUARTERS
    JQ = CH // P
    JH = TILES // 2
    PAIRS = QUARTERS // 2
    DIGITS = 2
    WORDS = P // DIGITS // 2
    HALF = D + 1
    COLS = 2 * HALF
    XC = 512
    XT = XC // P
    CHUNKS = N // XC
    GJ = 8
    NG = TILES // GJ
    SLOPE = 0.2
    EPS = 1e-5
    LO = 2.0 ** 11
    TOP = 2.0 ** 25
    MASK = 0x4040
    NEG_BYTE = 7
    STEPS0 = 8
    STEPS1 = 7

    adj_v = adj.rearrange("(t p) (q c) -> t p q c", p=P, q=QUARTERS)
    x_chunks = x.rearrange("(c k p) d -> c p k d", k=XT, p=P)
    XSLOTS = 4
    x_tiles = x.rearrange("(t p) d -> t p d", p=P)
    out_tiles = out.rearrange("(t p) d -> t p d", p=P)
    words_dram = nc.dram_tensor("words_dram", (TILES, P, TILES * WORDS // 2), U16, kind="Internal").ap()
    xh_dram = nc.dram_tensor("xh_dram", (TILES, P, 2 * D), F32, kind="Internal").ap()

    def row(dram, t):
        return dram[ds(t, 1)].rearrange("o p d -> p (o d)")

    ctx = ExitStack()
    with ctx:
        def sb(name, shape, dtype):
            return ctx.enter_context(nc.sbuf_tensor(name, shape, dtype))

        def pb(name, shape, dtype):
            return ctx.enter_context(nc.psum_tensor(name, shape, dtype))

        def sem(name):
            return ctx.enter_context(nc.semaphore(name))

        s2_row = sb("s2_row", [P, N], F32)
        wts_pos = sb("wts_pos", [P, TILES, COLS], F16)
        wts_neg = sb("wts_neg", [P, TILES, COLS], F16)
        adj_in = sb("adj_in", [P, QUARTERS, CH], I32)
        h1_all = adj_in[:, :, :].rearrange("p q c -> p (q c)").bitcast(F32).rearrange("p (t d) -> p t d", d=D)
        present = sb("present", [P, QUARTERS, CH], U8)
        words_in = present[:, :, :].rearrange("p q c -> p (q c)").bitcast(U16).rearrange(
            "p (s w) -> p s w", w=TILES * WORDS // 2)
        branch = sb("branch", [P, QUARTERS, CH], U8)
        words = sb("words", [P, 2, PAIRS, JQ, WORDS], U16)
        masks = sb("masks", [P, 2, 2, TILES, P], U8)
        h_all = wts_neg[:, :, :].rearrange("p t c -> p (t c)").bitcast(F32)[:, 0:TILES * D].rearrange(
            "p (t d) -> p t d", d=D)
        x_in = masks[:, 1].rearrange("p a t i -> p (a t i)").bitcast(F32)[:, 0:XSLOTS * XT * D].rearrange(
            "p (b k d) -> p b k d", b=XSLOTS, k=XT)
        scratch = sb("scratch", [P, 2, GJ * D], F32)
        xT_sb = scratch[:, :, 0:XC]
        acc = sb("acc", [P, 2, 2 * COLS], F32)
        early = NG // 2
        under_masks = masks[:, 1].rearrange("p a t i -> p (a t i)").bitcast(F32)
        slot_pos = scratch[:, 0, :]
        slot_neg = [under_masks[:, n * GJ * D:(n + 1) * GJ * D] for n in range(early)] + [
            (scratch[:, 1, :], acc[:, :, :].rearrange("p b c -> p (b c)")[:, 0:GJ * D])[n % 2]
            for n in range(early, NG)]
        slots1 = [wts_neg[:, :, :].rearrange("p t c -> p (t c)").bitcast(F32)[:, g * GJ * D:(g + 1) * GJ * D]
                  for g in range(NG)]
        x_res = sb("x_res", [P, 2, D], F32)
        xh = sb("xh", [P, 2, 2 * D], F32)
        total = sb("total", [P, COLS], F32)
        num = sb("num", [P, HALF], F32)
        guarded = sb("guarded", [P, HALF], F32)
        pre = sb("pre", [P, 2, D], F32)
        w0_sb = sb("w0_sb", [P, D], F32)
        h_rhs = sb("h_rhs", [P, D + 2], F32)
        b0_row = sb("b0_row", [P, D], F32)
        w1_sb = sb("w1_sb", [P, D], F32)
        eye_sb = sb("eye_sb", [P, P], F32)
        rep = sb("rep", [P, P], F32)
        x1T_sb = rep
        ones = w0_sb
        b1_row = sb("b1_row", [P, D], F32)
        wdst_row = sb("wdst_row", [P, D], F32)
        mean_row = sb("mean_row", [P, HALF], F32)
        hsum = h_rhs[:, 0:D]
        packer_sb = sb("packer_sb", [P, WORDS], dt.bfloat16)
        a12_sb = sb("a12_sb", [P, 2], F32)
        b0_sb = sb("b0_sb", [P, 1], F32)
        dn = sb("dn", [P, 2, TILES, 2], F16)
        ba_sb = sb("ba_sb", [P, 1], F32)
        s12 = sb("s12", [P, TILES, 2], F32)
        s_dst = sb("s_dst", [P, TILES], F32)
        thr = sb("thr", [P, TILES], F32)
        zM = sb("zM", [P, TILES], F32)
        zlow = sb("zlow", [P, TILES], F32)
        alpha = sb("alpha", [P, TILES], F32)
        beta = sb("beta", [P, TILES], F32)
        v = sb("v", [P, 2, TILES], F32)
        vK = sb("vK", [P, 2, TILES], F32)
        vD = total[:, 0:2 * TILES].rearrange("p (k t) -> p k t", k=2)
        chunk_stats = sb("chunk_stats", [P, 2, CHUNKS], F32)
        hmax_t = sb("hmax_t", [P, TILES], F32)
        cst = sb("cst", [P, 10], F32)
        sig_bias = sb("sig_bias", [P, 1], F32)
        eps = sb("eps", [P, 1], F32)
        minus_half = sb("minus_half", [P, 1], F32)
        iszero = sb("iszero", [P, 1], F32)
        rden = sb("rden", [P, 2], F32)
        bn = sb("bn", [P, 6], F32)
        mv = sb("mv", [P, 2, 2], F32)
        veps = sb("veps", [P, 1], F32)
        rstd = sb("rstd", [P, 2], F32)

        psum = pb("psum", [P, 8, 512], F32)
        bank = [psum[:, i, :] for i in range(8)]
        acc_ps = [(bank[0], bank[1]), (bank[2], bank[3])]
        pack_ps = [bank[4], bank[5]]
        x1T_ps, h1_ps = bank[6], bank[7]
        xT_ps, s2_ps, small_ps = bank[0:2], bank[6:8], bank[7]

        def h_ps(b):
            return psum[:, 2 + 2 * b:4 + 2 * b, 0:2 * (D + 2)].rearrange("p n (k c) -> p n k c", c=D + 2)

        const_in, eye_in, later_in = sem("const_in"), sem("eye_in"), sem("later_in")
        dve_const = sem("dve_const")
        x_in_landed = [sem(f"x_in_landed{k}") for k in range(XSLOTS)]
        small_done, h_rhs_ready = sem("small_done"), sem("h_rhs_ready")
        xT_done, xT_copied = sem("xT_done"), sem("xT_copied")
        h_done, h_added, h_out = sem("h_done"), sem("h_added"), sem("h_out")
        s2_done, s2_copied = sem("s2_done"), sem("s2_copied")
        setup = sem("setup")
        hmax_in, hmax_out = sem("hmax_in"), sem("hmax_out")
        xsum_ready, hsum_done = sem("xsum_ready"), sem("hsum_done")
        exp_in, exp_out = sem("exp_in"), sem("exp_out")
        y_pos, y_neg = sem("y_pos"), sem("y_neg")
        hi_pos, hi_neg = sem("hi_pos"), sem("hi_neg")
        lo_pos, left_neg, lo_neg = sem("lo_pos"), sem("left_neg"), sem("lo_neg")
        den_step = sem("den_step")
        adj_landed = [sem(f"adj_landed{q}") for q in range(QUARTERS)]
        pairs_made = sem("pairs_made")
        present_made, branch_made, edges_made = sem("present_made"), sem("branch_made"), sem("edges_made")
        packed, words_made = sem("packed"), sem("words_made")
        words_stored = [sem("words_stored0"), sem("words_stored1")]
        masks_made, acc_done, acc_copied = sem("masks_made"), sem("acc_done"), sem("acc_copied")
        x_res_landed = [sem("x_res_landed0"), sem("x_res_landed1")]
        fold, stats_made, veps_made, rstd_made = sem("fold"), sem("stats_made"), sem("veps_made"), sem("rstd_made")
        x1_made, x1T_done, x1T_copied, h1_done = sem("x1_made"), sem("x1T_done"), sem("x1T_copied"), sem("h1_done")
        h1_biased, h1_made, hsum_added = sem("h1_biased"), sem("h1_made"), sem("hsum_added")
        xh_stored = [sem("xh_stored0"), sem("xh_stored1")]
        h1_in = [sem(f"h1_in{g}") for g in range(NG)]
        max1_in, max1_out = sem("max1_in"), sem("max1_out")
        y1, hi1, lo1 = sem("y1"), sem("hi1"), sem("lo1")
        y1_pool, left1, lo1_pool = sem("y1_pool"), sem("left1"), sem("lo1_pool")
        words_landed = [sem("words_landed0"), sem("words_landed1")]
        any_made, masks1_made, acc1_done, acc1_copied = sem("any_made"), sem("masks1_made"), sem("acc1_done"), sem("acc1_copied")
        x1_landed = [sem("x1_landed0"), sem("x1_landed1")]
        fold1, stats1, veps1, rstd1, out_made = sem("fold1"), sem("stats1"), sem("veps1"), sem("rstd1"), sem("out_made")
        out_stored = [sem("out_stored0"), sem("out_stored1")]

        act_passed, dve_passed, pe_passed = sem("act_passed"), sem("dve_passed"), sem("pe_passed")

        block = ctx.enter_context(nc.Block())
        CONSTS = 6
        LATER = 4

        def product(engine, slot, vkind, g, src):
            return engine.tensor_tensor(
                slot.rearrange("p (j d) -> p j d", d=D), src[:, GJ * g:GJ * (g + 1), :],
                vK[:, vkind, GJ * g:GJ * (g + 1)].unsqueeze(2).to_broadcast([P, GJ, D]), ALU.mult)

        def denominator_columns(engine, wts, vkind, g):
            return engine.tensor_copy(wts[:, GJ * g:GJ * (g + 1), :].rearrange("p j (s c) -> p j s c", s=2)[:, :, :, D],
                                      dn[:, vkind, GJ * g:GJ * (g + 1), :])

        def high_half(wts, slot, g, scale):
            return nc.scalar.mul(wts[:, GJ * g:GJ * (g + 1), 0:D], slot.rearrange("p (j d) -> p j d", d=D), scale)

        def low_half(wts, slot, g):
            denominator_columns(nc.vector, wts, 0, g)
            return nc.vector.scalar_tensor_tensor(
                wts[:, GJ * g:GJ * (g + 1), HALF:HALF + D], wts[:, GJ * g:GJ * (g + 1), 0:D], -LO,
                slot.rearrange("p (j d) -> p j d", d=D), ALU.mult, ALU.add)

        def left_over(wts, slot, g):
            blocks = slot.rearrange("p (j d) -> p j d", d=D)
            return nc.gpsimd.tensor_tensor(blocks, blocks, wts[:, GJ * g:GJ * (g + 1), 0:D], ALU.subtract)

        def low_from_left_over(wts, slot, g):
            return nc.scalar.mul(wts[:, GJ * g:GJ * (g + 1), HALF:HALF + D], slot.rearrange("p (j d) -> p j d", d=D), LO)

        def pieces_of(n):
            tile, n = 1 + n // early, n % early
            return [(tile, q) for q in range(QUARTERS * n // early, QUARTERS * (n + 1) // early) if tile >= 1]

        pool_groups = [g for g in range(NG) if g % 3 == 2 or g == NG - 1]
        dve_groups = [g for g in range(NG) if g not in pool_groups]

        def mask1(t, b):
            return masks[:, 1 if isinstance(t, int) and t in (2, 3) else 0, b]

        @block.sync
        def _(sp):
            for k in range(XSLOTS):
                if k == 2:
                    sp.wait_ge(const_in, 16 * CONSTS)
                sp.dma_start(x_in[:, k], x_chunks[k]).then_inc(x_in_landed[k], 16)
            with sp.Fori(1, CHUNKS // XSLOTS) as u:
                for k in range(XSLOTS):
                    sp.wait_ge(xT_done, XSLOTS * u - XSLOTS + k + 1)
                    sp.dma_start(x_in[:, k], x_chunks[ds(XSLOTS * u + k, 1)].rearrange(
                        "o p k d -> p (o k) d")).then_inc(x_in_landed[k], 16)

            def feed(t):
                for q in range(QUARTERS):
                    sp.wait_ge(present_made, 4 * (t - 1) + q + 1)
                    sp.dma_start(adj_in[:, q, :], adj_v[ds(t, 1), :, q, :].rearrange(
                        "o p c -> p (o c)")).then_inc(adj_landed[q], 16)

            def residual(t, b, first=False):
                if not first:
                    sp.wait_ge(fold, STEPS0 * (t - 1))
                sp.dma_start(x_res[:, b, :], row(x_tiles, t)).then_inc(x_res_landed[b], 16)

            def store_words(t, b):
                sp.wait_ge(words_made, 2 * t + 2)
                sp.dma_start(row(words_dram, t), words[:, b].rearrange("p h t w -> p (h t w)")).then_inc(
                    words_stored[b], 16)

            def store_xh(t, b):
                sp.wait_ge(h1_made, t + 1)
                sp.dma_start(row(xh_dram, t), xh[:, b, :]).then_inc(xh_stored[b], 16)

            feed(1)
            feed(2)
            store_words(0, 0)
            for t in range(2):
                residual(t, t, first=True)
                feed(t + 3)
                store_words(t + 1, (t + 1) % 2)
            with sp.Fori(0, (TILES - 6) // 2) as u:
                for k in range(2):
                    t = 2 * u + k + 2
                    residual(t, k)
                    store_xh(t - 2, k)
                    feed(t + 3)
                    store_words(t + 1, 1 - k)
            for t in range(TILES - 4, TILES):
                residual(t, t % 2)
                store_xh(t - 2, t % 2)
                if t + 3 < TILES:
                    feed(t + 3)
                if t + 1 < TILES:
                    store_words(t + 1, (t + 1) % 2)
            sp.wait_ge(present_made, 4 * TILES)

            def load_h1(g):
                sp.dma_start(h1_all[:, GJ * g:GJ * (g + 1), :],
                             xh_dram[GJ * g:GJ * (g + 1), :, D:2 * D].rearrange("t p d -> p t d")).then_inc(
                    h1_in[g], 16)

            def load_words(t, b, first=False):
                if not first:
                    sp.wait_ge(any_made, t - 1)
                sp.dma_start(words_in[:, b, :], row(words_dram, t)).then_inc(words_landed[b], 16)

            def load_x1(t, b, first=False):
                if first:
                    sp.wait_ge(fold, STEPS0 * (TILES - 1 + b))
                else:
                    sp.wait_ge(fold1, STEPS1 * (t - 1))
                sp.dma_start(x_res[:, b, :], xh_dram[ds(t, 1), :, 0:D].rearrange(
                    "o p d -> p (o d)")).then_inc(x1_landed[b], 16)

            def store_out(t, b):
                sp.wait_ge(out_made, t + 1)
                sp.dma_start(row(out_tiles, t), xh[:, b, 0:D]).then_inc(out_stored[b], 16)

            for b in range(2):
                sp.wait_ge(words_stored[b], 16 * JH)
            sp.wait_ge(edges_made, 4 * TILES)
            for t in range(2):
                load_words(t, t, first=True)
            sp.wait_ge(xh_stored[0], 16 * (JH - 1))
            sp.wait_ge(xh_stored[1], 16 * (JH - 1))
            for g in range(NG - 1):
                load_h1(g)
            for t in range(TILES - 2, TILES):
                store_xh(t, t % 2)
            for b in range(2):
                sp.wait_ge(xh_stored[b], 16 * JH)
            load_h1(NG - 1)
            for t in range(2):
                load_x1(t, t, first=True)
            for t in (0, 1):
                load_words(t + 2, t)
            with sp.Fori(0, (TILES - 4) // 2) as u:
                for b in range(2):
                    t = 2 * u + b + 2
                    load_words(t + 2, b)
                    load_x1(t, b)
                    store_out(t - 2, b)
            for t in range(TILES - 2, TILES):
                load_x1(t, t % 2)
                store_out(t - 2, t % 2)
            for t in range(TILES - 2, TILES):
                store_out(t, t % 2)
            for b in range(2):
                sp.wait_ge(out_stored[b], 16 * JH)

        @block.scalar
        def _(act):
            for dst, src, landed in (
                (eye_sb[:, :], eye, eye_in),
                (w0_sb[:, :], w0, const_in), (a12_sb[:, :], a12, const_in), (b0_sb[:, :], b0_col, const_in),
                (ba_sb[:, :], ba.to_broadcast([P, 1]), const_in), (h_rhs[:, 0:D], w0t, const_in),
                (b0_row[:, :], b0.to_broadcast([P, D]), const_in),
                (packer_sb[:, :], packer, later_in), (w1_sb[:, :], w1, later_in),
                (b1_row[:, :], b1.to_broadcast([P, D]), later_in),
                (wdst_row[:, :], watt[:, D:2 * D].to_broadcast([P, D]), later_in),
            ):
                act.dma_start(dst, src).then_inc(landed, 16)

            def copy_xT(c, b, first=False):
                act.wait_ge(xT_done, c + 1)
                if not first:
                    act.wait_ge(s2_done, c - 1)
                nc.scalar.activation(xT_sb[:, b, :], xT_ps[b], ACT.Identity,
                                     accum_out=chunk_stats[:, 1, ds(c, 1)]).then_inc(xT_copied, 1)

            def copy_s2(c, b):
                act.wait_ge(s2_done, c + 1)
                nc.scalar.copy(s2_row[:, ds(c * XC, XC)], s2_ps[b]).then_inc(s2_copied, 1)

            def make_present(t, q, nth):
                act.wait_ge(adj_landed[q], 16 * t + 16)
                if nth:
                    act.wait_ge(edges_made, 4 * t - 4 + q + 1)
                act.sem_inc(act_passed, 1)
                nc.scalar.activation(present[:, q, :].bitcast(F8), adj_in[:, q, :], ACT.Sigmoid,
                                     bias=sig_bias[:, 0:1], scale=64.0, saturate=False).then_inc(present_made, 1)

            copy_xT(0, 0, first=True)
            copy_xT(1, 1, first=True)
            copy_s2(0, 0)
            for q in range(QUARTERS):
                first, last = max(1, q * CHUNKS // 8), (q + 1) * CHUNKS // 8
                if first < last:
                    with act.Fori(first, last) as u:
                        for b in range(2):
                            copy_xT(2 * u + b, b)
                            copy_s2(2 * u + b - 1, 1 - b)
                act.dma_start(adj_in[:, q, :], adj_v[0, :, q, :]).then_inc(adj_landed[q], 16)
                if q:
                    make_present(0, q - 1, 0)
            copy_s2(CHUNKS - 1, 1)
            make_present(0, QUARTERS - 1, 0)
            def copy_words(t, b, half, free=None):
                act.wait_ge(packed, 2 * t + half + 1)
                if free is not None:
                    act.wait_ge(masks_made, t - 1)
                    act.wait_ge(words_stored[b], 16 * free)
                nc.scalar.copy(words[:, b, half],
                               pack_ps[half][:, 0:JQ * WORDS].rearrange("p (j w) -> p j w", w=WORDS)).then_inc(
                    words_made, 1)

            copy_words(0, 0, 0)
            nc.scalar.activation(veps[:, :], sig_bias[:, 0:1], ACT.Exp)
            copy_words(0, 0, 1)
            act.wait_ge(exp_in, 1)
            nc.scalar.activation(v[:, 0, :], s12[:, :, 1], ACT.Exp, bias=cst[:, 3:4])
            nc.scalar.activation(v[:, 1, :], s12[:, :, 1], ACT.Exp, bias=cst[:, 4:5], scale=SLOPE)
            nc.scalar.activation(alpha[:, :], zM[:, :], ACT.Exp)
            nc.scalar.activation(beta[:, :], zlow[:, :], ACT.Exp).then_inc(exp_out, 1)

            def copy_acc(t, b, older=True):
                act.wait_ge(acc_done, t + 1)
                if older:
                    act.wait_ge(fold, STEPS0 * (t - 2) + 1 if not isinstance(t, int) or t > 1 else 1)
                nc.scalar.mul(acc[:, b, 0:COLS], acc_ps[b][0][:, 0:COLS], alpha[:, ds(t, 1)])
                nc.scalar.mul(acc[:, b, COLS:2 * COLS], acc_ps[b][1][:, 0:COLS], beta[:, ds(t, 1)]).then_inc(
                    acc_copied, 1)

            def copy_x1T(t):
                act.wait_ge(x1T_done, t + 1)
                nc.scalar.copy(x1T_sb[:, :], x1T_ps[:, 0:P]).then_inc(x1T_copied, 1)

            def hi_halves(n):
                g = NG - 1 - n
                act.wait_ge(y_pos, n + 1)
                act.wait_ge(y_neg, n + 1)
                high_half(wts_neg, slot_neg[n], g, 1.0).then_inc(hi_neg, 1)
                high_half(wts_pos, slot_pos, g, 1.0 / LO).then_inc(hi_pos, 1)

            def lo_half(n):
                act.wait_ge(left_neg, n + 1)
                low_from_left_over(wts_neg, slot_neg[n], NG - 1 - n).then_inc(lo_neg, 1)

            for n in range(NG):
                hi_halves(n)
                if n:
                    lo_half(n - 1)
                if n == early:
                    copy_words(1, 1, 0)
                    copy_words(1, 1, 1)
                for tile, q in pieces_of(n):
                    make_present(tile, q, 1)
            lo_half(NG - 1)
            copy_words(2, 0, 0, 1)
            copy_words(2, 0, 1, 1)
            copy_acc(0, 0, older=False)
            for q in range(QUARTERS):
                make_present(3, q, 1)
            copy_x1T(0)

            def iteration(t, b, free, last=False, older=True):
                copy_acc(t - 1, 1 - b, older)
                if not last:
                    make_present(t + 2, 0, 1)
                copy_words(t + 1, 1 - b, 0, free)
                if not last:
                    make_present(t + 2, 1, 1)
                copy_words(t + 1, 1 - b, 1, free)
                copy_x1T(t - 1)
                if not last:
                    make_present(t + 2, 2, 1)
                    make_present(t + 2, 3, 1)

            iteration(2, 0, 1, older=False)
            with act.Fori(0, (TILES - 6) // 2) as u:
                for k in range(2):
                    t = 2 * u + k + 3
                    iteration(t, 1 - k, u + 2)
            iteration(TILES - 3, 1, JH - 1)
            iteration(TILES - 2, 0, JH - 1, last=True)
            copy_acc(TILES - 2, 0)
            copy_x1T(TILES - 2)
            copy_acc(TILES - 1, 1)
            copy_x1T(TILES - 1)

            act.wait_ge(max1_out, 3)
            nc.scalar.activation(v[:, 0, :], s_dst[:, :], ACT.Exp, bias=cst[:, 3:4]).then_inc(exp_out, 1)
            def lo_half1(g):
                act.wait_ge(left1, pool_groups.index(g) + 1)
                low_from_left_over(wts_pos, slots1[g], g).then_inc(lo1_pool, 1)

            for g in range(NG):
                if g in pool_groups:
                    act.wait_ge(y1_pool, pool_groups.index(g) + 1)
                    high_half(wts_pos, slots1[g], g, 1.0).then_inc(hi1, 1)
                else:
                    act.wait_ge(y1, dve_groups.index(g) + 1)
                    high_half(wts_pos, slots1[g], g, 1.0 / LO).then_inc(hi1, 1)
                if g - 1 in pool_groups:
                    lo_half1(g - 1)
            lo_half1(NG - 1)

            def copy_acc1(t, b, older=True):
                act.wait_ge(acc1_done, t + 1)
                if older:
                    act.wait_ge(fold1, STEPS1 * (t - 2) + 1)
                nc.scalar.copy(acc[:, b, 0:COLS], acc_ps[b][0][:, 0:COLS]).then_inc(acc1_copied, 1)

            copy_acc1(0, 0, older=False)
            copy_acc1(1, 1, older=False)
            with act.Fori(1, JH) as u:
                for b in range(2):
                    copy_acc1(2 * u + b, b)

        @block.vector
        def _(dve):
            nc.vector.memset(sig_bias[:, :], -32.0)
            nc.vector.memset(minus_half[:, :], -0.5)
            nc.vector.memset(eps[:, :], EPS)
            dve.wait_ge(const_in, 16 * CONSTS)
            nc.vector.tensor_copy(rep[:, :], b0_sb[:, 0:1].to_broadcast([P, P])).then_inc(dve_const, 1)
            dve.wait_ge(small_done, 1)
            nc.vector.tensor_copy(h_rhs[:, D:D + 2], small_ps[:, 0:2])
            nc.vector.tensor_copy(rep[:, :], small_ps[:, 1:2].to_broadcast([P, P]))
            nc.vector.memset(ones[:, :], 1.0)
            nc.vector.tensor_tensor(cst[:, 8:9], small_ps[:, 2:3], ba_sb[:, 0:1], ALU.add).then_inc(h_rhs_ready, 1)
            dve.wait_ge(h_rhs_ready, 1)
            nc.vector.tensor_tensor(cst[:, 9:10], small_ps[:, 3:4], cst[:, 8:9], ALU.add).then_inc(h_rhs_ready, 1)

            def take_h(c, b):
                dve.wait_ge(h_done, c + 1)
                nc.vector.tensor_copy(
                    s12[:, ds(c * XT, XT), :].rearrange("p (n k) c -> p n k c", n=2), h_ps(b)[:, :, :, D:D + 2])
                nc.vector.tensor_tensor(
                    h_all[:, ds(c * XT, XT), :].rearrange("p (n k) d -> p n k d", n=2), h_ps(b)[:, :, :, 0:D],
                    b0_row[:, :].unsqueeze(1).unsqueeze(1).to_broadcast([P, 2, 2, D]), ALU.add).then_inc(h_out, 1)

            def make_branch(t, q, older=True):
                if older:
                    dve.wait_ge(packed, 2 * t - 2 + q // 2 + 1)
                nc.vector.tensor_scalar(branch[:, q, :], s2_row[:, q * CH:(q + 1) * CH],
                                        thr[:, ds(t, 1)], NEG_BYTE, ALU.is_gt, ALU.add).then_inc(
                    branch_made, 1)

            def make_edges(t, q):
                dve.wait_ge(branch_made, 4 * t + q + 1)
                dve.wait_ge(present_made, 4 * t + q + 1)
                nc.vector.scalar_tensor_tensor(branch[:, q, :].bitcast(U32), present[:, q, :].bitcast(U32), 1,
                                               branch[:, q, :].bitcast(U32), ALU.logical_shift_right,
                                               ALU.bitwise_and).then_inc(edges_made, 1)
                if q % 2:
                    dve.wait_ge(edges_made, 4 * t + q + 1)
                    nc.vector.scalar_tensor_tensor(branch[:, q - 1, :].bitcast(U32), branch[:, q - 1, :].bitcast(U32), 2,
                                                   branch[:, q, :].bitcast(U32), ALU.logical_shift_right,
                                                   ALU.bitwise_or).then_inc(pairs_made, 1)

            TQ = TILES // QUARTERS
            for q in range(QUARTERS):
                with dve.Fori(q * CHUNKS // 8, (q + 1) * CHUNKS // 8) as u:
                    for b in range(2):
                        take_h(2 * u + b, b)
                dve.wait_ge(h_out, (q + 1) * CHUNKS // 4)
                nc.vector.tensor_scalar(thr[:, q * TQ:(q + 1) * TQ], s12[:, q * TQ:(q + 1) * TQ, 0], cst[:, 9:10], -1.0,
                                        ALU.add, ALU.mult).then_inc(h_added, 1)
                nc.vector.tensor_reduce(chunk_stats[:, 0, q:q + 1],
                                        h_all[:, q * TQ:(q + 1) * TQ, :].rearrange("p k d -> p (k d)"), AX.X, ALU.max,
                                        apply_absolute_value=True).then_inc(h_added, 1)
                if q:
                    dve.wait_ge(h_added, 2 * q)
                    dve.wait_ge(s2_copied, q * CHUNKS // 4)
                    make_branch(0, q - 1, older=False)
                    make_edges(0, q - 1)

            steps = [0]

            def step(ins):
                steps[0] += 1
                ins.then_inc(setup, 1)
                dve.wait_ge(setup, steps[0])

            dve.wait_ge(h_added, 2 * QUARTERS)
            nc.vector.tensor_reduce(cst[:, 1:2], chunk_stats[:, 0, 0:QUARTERS], AX.X, ALU.max)
            nc.vector.tensor_reduce(cst[:, 0:1], s12[:, :, 1], AX.X, ALU.max).then_inc(hmax_in, 1)
            dve.wait_ge(s2_copied, CHUNKS)
            make_branch(0, QUARTERS - 1, older=False)
            make_edges(0, QUARTERS - 1)
            dve.wait_ge(xT_copied, CHUNKS)
            step(nc.vector.tensor_reduce(cst[:, 2:3], chunk_stats[:, 1, :], AX.X, ALU.add))
            dve.wait_ge(hmax_out, 1)
            nc.vector.tensor_scalar(cst[:, 3:4], cst[:, 0:1], -1.0, None, ALU.mult)
            nc.vector.tensor_scalar(cst[:, 4:5], cst[:, 0:1], -SLOPE, None, ALU.mult)
            step(nc.vector.tensor_scalar(zM[:, :], s12[:, :, 0], cst[:, 9:10], cst[:, 0:1], ALU.add, ALU.add))
            step(nc.vector.scalar_tensor_tensor(zlow[:, :], zM[:, :], SLOPE, zM[:, :], ALU.mult, ALU.max))
            step(nc.vector.tensor_tensor(alpha[:, :], zM[:, :], zlow[:, :], ALU.subtract))
            step(nc.vector.scalar_tensor_tensor(zlow[:, :], zM[:, :], SLOPE, zlow[:, :], ALU.mult, ALU.subtract))
            nc.vector.tensor_copy(zM[:, :], alpha[:, :]).then_inc(exp_in, 1)

            def scales(layer_done):
                step(nc.vector.tensor_scalar(cst[:, 5:6], cst[:, 1:2], 1e-30, None, ALU.max))
                step(nc.vector.tensor_scalar(cst[:, 5:6].bitcast(I32), cst[:, 5:6].bitcast(I32), 0x7F800000,
                                             None, ALU.bitwise_and))
                step(nc.vector.reciprocal(cst[:, 6:7], cst[:, 5:6]))
                nc.vector.tensor_scalar(cst[:, 8:9], cst[:, 6:7], 1.0 / N, None, ALU.mult)
                step(nc.vector.tensor_scalar(cst[:, 7:8], cst[:, 6:7], TOP, None, ALU.mult))

            def scaled_v(kinds):
                for kind in range(2):
                    vkind = kind if kind in kinds else 0
                    if kind:
                        nc.vector.tensor_scalar(vK[:, 1, :], v[:, vkind, :], cst[:, 7:8], 1.0 / LO, ALU.mult, ALU.mult)
                    else:
                        nc.vector.tensor_scalar(vK[:, 0, :], v[:, 0, :], cst[:, 7:8], None, ALU.mult)
                for kind in kinds:
                    nc.vector.tensor_scalar(vD[:, kind, :], v[:, kind, :], TOP, None, ALU.mult).then_inc(den_step, 1)
                den_steps[0] += len(kinds)
                dve.wait_ge(den_step, den_steps[0])

            def denominators(kinds):
                for kind in kinds:
                    nc.vector.tensor_scalar(dn[:, kind, :, 0], vD[:, kind, :], 1.0 / LO, None, ALU.mult).then_inc(den_step, 1)
                dve.wait_ge(den_step, den_steps[0] + len(kinds))
                for kind in kinds:
                    nc.vector.scalar_tensor_tensor(dn[:, kind, :, 1], dn[:, kind, :, 0], -LO, vD[:, kind, :],
                                                   ALU.mult, ALU.add).then_inc(den_step, 1)
                den_steps[0] += 2 * len(kinds)
                dve.wait_ge(den_step, den_steps[0])

            def pieces(t, first=0, last=QUARTERS):
                make_branch(t, first)
                for q in range(first + 1, last):
                    make_branch(t, q)
                    make_edges(t, q - 1)
                make_edges(t, last - 1)

            def unpack(src, dst, odd):
                to = dst.bitcast(U16).rearrange("p (h e j) i -> p h e j i", h=PAIRS, e=2)
                for k in range(DIGITS):
                    for e in range(2):
                        left = 6 - 4 * k - 2 * e - odd
                        last = nc.vector.tensor_scalar(
                            to[:, :, e, :, WORDS * k:WORDS * (k + 1)], src, abs(left), MASK,
                            ALU.logical_shift_left if left >= 0 else ALU.logical_shift_right, ALU.bitwise_and)
                return last

            def make_masks(t, b, older=True):
                dve.wait_ge(words_made, 2 * t + 2)
                if older:
                    dve.wait_ge(acc_done, t - 1)
                unpack(words[:, b], masks[:, b, 1], 0)
                unpack(words[:, b], masks[:, b, 0], 1).then_inc(masks_made, 1)

            den_steps = [0]
            scales(0)
            dve.wait_ge(exp_out, 1)
            scaled_v((0, 1))
            denominators((0, 1))

            def fold_tile(done, t, b, two_branches, copied, landed, nth, stats):
                n = [0]
                count = STEPS0 if two_branches else STEPS1

                def chained(ins):
                    n[0] += 1
                    ins.then_inc(done, 1)
                    dve.wait_ge(done, count * t + n[0])

                dve.wait_ge(copied, t + 1)
                src = acc[:, b, 0:COLS]
                if two_branches:
                    chained(nc.vector.tensor_tensor(total[:, :], acc[:, b, 0:COLS], acc[:, b, COLS:2 * COLS], ALU.add))
                    src = total[:, :]
                chained(nc.vector.scalar_tensor_tensor(num[:, :], src[:, HALF:COLS], 1.0 / LO, src[:, 0:HALF],
                                                       ALU.mult, ALU.add))
                chained(nc.vector.tensor_scalar(iszero[:, :], num[:, D:HALF], 0.0, None, ALU.is_equal))
                chained(nc.vector.scalar_tensor_tensor(guarded[:, :], mean_row[:, :], iszero[:, 0:1], num[:, :],
                                                       ALU.mult, ALU.add))
                chained(nc.vector.reciprocal(rden[:, 0:1], guarded[:, D:HALF]))
                chained(nc.vector.tensor_scalar(rden[:, 1:2], rden[:, 0:1], cst[:, 5:6], None, ALU.mult))
                dve.wait_ge(landed, nth)
                chained(nc.vector.scalar_tensor_tensor(pre[:, b, :], guarded[:, 0:D], rden[:, 1:2], x_res[:, b, :],
                                                       ALU.mult, ALU.add))
                chained(nc.vector.bn_stats(bn[:, :], pre[:, b, :]))
                dve.sem_inc(dve_passed, 1)
                nc.vector.bn_aggr(mv[:, b, :], bn[:, :]).then_inc(stats, 1)

            def normalise(t, b, ready, made, stored, nth):
                dve.wait_ge(ready, t + 1)
                if nth is not None:
                    dve.wait_ge(stored, nth)
                nc.vector.tensor_scalar(xh[:, b, 0:D], pre[:, b, :], mv[:, b, 0:1], rstd[:, b:b + 1],
                                        ALU.subtract, ALU.mult).then_inc(made, 1)

            def finish_h1(t, b, older=True):
                dve.wait_ge(h1_done, t + 1)
                if older:
                    dve.wait_ge(hsum_added, t)
                nc.vector.tensor_tensor(xh[:, b, D:2 * D], h1_ps[:, 0:D], b1_row[:, :], ALU.add).then_inc(h1_biased, 1)
                dve.wait_ge(h1_biased, t + 1)
                nc.vector.scalar_tensor_tensor(num[:, 0:D], xh[:, b, D:2 * D], 1.0, wdst_row[:, :], ALU.mult,
                                               ALU.mult, accum_out=s_dst[:, ds(t, 1)])
                nc.vector.tensor_reduce(hmax_t[:, ds(t, 1)], xh[:, b, D:2 * D], AX.X, ALU.max,
                                        apply_absolute_value=True).then_inc(h1_made, 1)

            for n in range(NG):
                g = NG - 1 - n
                if n >= 1:
                    dve.wait_ge(lo_pos, n)
                product(nc.vector, slot_pos, 0, g, h_all).then_inc(y_pos, 1)
                if n == 0:
                    nc.vector.tensor_scalar(rep[:, :], ones[:, :], cst[:, 2:3], None, ALU.mult).then_inc(xsum_ready, 1)
                if n == 1:
                    make_masks(0, 0, older=False)
                for piece in pieces_of(n - 1):
                    make_edges(*piece)
                for piece in pieces_of(n):
                    make_branch(*piece)
                dve.wait_ge(hi_pos, n + 1)
                low_half(wts_pos, slot_pos, g).then_inc(lo_pos, 1)
                if n == early:
                    dve.wait_ge(lo_neg, early)
                    make_masks(1, 1, older=False)
            for piece in pieces_of(NG - 1):
                make_edges(*piece)
            dve.wait_ge(hsum_done, 1)
            nc.vector.memset(mean_row[:, D:HALF], 1.0)
            step(nc.vector.scalar_tensor_tensor(mean_row[:, 0:D], small_ps[:, 0:D], 1.0 / N, b0_row[:, :],
                                                ALU.mult, ALU.add))
            step(nc.vector.tensor_scalar(mean_row[:, 0:D], mean_row[:, 0:D], cst[:, 6:7], None, ALU.mult))
            make_masks(2, 0)
            pieces(3, 0, QUARTERS // 2)
            fold_tile(fold, 0, 0, True, acc_copied, x_res_landed[0], 16, stats_made)
            normalise(0, 0, rstd_made, x1_made, xh_stored[0], None)

            def iteration(t, b, nth, first_piece=0, last=False):
                if not last:
                    pieces(t + 1, first_piece)
                fold_tile(fold, t - 1, 1 - b, True, acc_copied, x_res_landed[1 - b], 16 * nth, stats_made)
                if not isinstance(t, int) or t >= 2:
                    finish_h1(t - 2, b, older=not isinstance(t, int) or t >= 3)
                normalise(t - 1, 1 - b, rstd_made, x1_made, xh_stored[1 - b],
                          None if isinstance(t, int) and t < 3 else 16 * (nth - 1))
                if not last:
                    make_masks(t + 1, 1 - b)

            iteration(2, 0, 1, QUARTERS // 2)
            with dve.Fori(0, (TILES - 4) // 2) as u:
                for k in range(2):
                    iteration(2 * u + k + 3, 1 - k, u + 2)
            iteration(TILES - 1, 1, JH, last=True)

            def make_masks1(t, b, older=True, nth=None):
                dve.wait_ge(words_landed[b], nth)
                flat = words[:, b].rearrange("p h t w -> p (h t w)")
                nc.vector.scalar_tensor_tensor(flat, words_in[:, b, :], 1, words_in[:, b, :],
                                               ALU.logical_shift_right, ALU.bitwise_or).then_inc(any_made, 1)
                dve.wait_ge(any_made, t + 1)
                if older:
                    dve.wait_ge(acc1_done, t - 1)
                elif t < 2:
                    dve.wait_ge(acc_done, TILES - 1)
                unpack(words[:, b], mask1(t, b), 0).then_inc(masks1_made, 1)

            make_masks1(0, 0, older=False, nth=16)
            make_masks1(1, 1, older=False, nth=16)
            fold_tile(fold, TILES - 1, 1, True, acc_copied, x_res_landed[1], 16 * JH, stats_made)
            finish_h1(TILES - 2, 0)
            normalise(TILES - 1, 1, rstd_made, x1_made, xh_stored[1], 16 * (JH - 1))
            finish_h1(TILES - 1, 1)

            dve.wait_ge(h1_made, TILES)
            nc.vector.tensor_reduce(cst[:, 0:1], s_dst[:, :], AX.X, ALU.max)
            nc.vector.tensor_reduce(cst[:, 1:2], hmax_t[:, :], AX.X, ALU.max).then_inc(max1_in, 1)
            dve.wait_ge(max1_out, 1)
            nc.vector.tensor_scalar(cst[:, 3:4], cst[:, 0:1], -1.0, None, ALU.mult).then_inc(max1_out, 2)
            scales(1)
            dve.wait_ge(exp_out, 2)
            scaled_v((0,))

            def low1(g):
                dve.wait_ge(hi1, g + 1)
                low_half(wts_pos, slots1[g], g).then_inc(lo1, 1)

            for n, g in enumerate(dve_groups):
                dve.wait_ge(h1_in[g], 16)
                product(nc.vector, slots1[g], 0, g, h1_all).then_inc(y1, 1)
                if n == 0:
                    denominators((0,))
                if n:
                    low1(dve_groups[n - 1])
            low1(dve_groups[-1])
            dve.wait_ge(hsum_done, 2)
            nc.vector.tensor_scalar(mean_row[:, 0:D], h1_ps[:, 0:D], cst[:, 8:9], None, ALU.mult)

            def iteration1(t, b, nth, nth_w, last=False, older=True):
                if not last:
                    make_masks1(t + 1, 1 - b, older=not isinstance(t, int) or t > 2, nth=nth_w)
                fold_tile(fold1, t - 1, 1 - b, False, acc1_copied, x1_landed[1 - b], 16 * nth, stats1)
                normalise(t - 1, 1 - b, rstd1, out_made, out_stored[1 - b], 16 * (nth - 1) if older else None)

            iteration1(1, 1, 1, 32, older=False)
            iteration1(2, 0, 1, 32, older=False)
            with dve.Fori(0, (TILES - 4) // 2) as u:
                for k in range(2):
                    iteration1(2 * u + k + 3, 1 - k, u + 2, 16 * u + 48)
            iteration1(TILES - 1, 1, JH, None, last=True)
            iteration1(TILES, 0, JH, None, last=True)

        @block.gpsimd
        def _(pool):
            pool.wait_ge(hmax_in, 1)
            nc.gpsimd.partition_all_reduce(cst[:, 0:2], cst[:, 0:2], P, MAX).then_inc(hmax_out, 1)
            pool.wait_ge(den_step, 6)
            def subtract_neg(n):
                g = NG - 1 - n
                pool.wait_ge(hi_neg, n + 1)
                denominator_columns(nc.gpsimd, wts_neg, 1, g)
                left_over(wts_neg, slot_neg[n], g).then_inc(left_neg, 1)

            for n in range(NG):
                if n >= early + 2:
                    pool.wait_ge(lo_neg, n - 1)
                product(nc.gpsimd, slot_neg[n], 1, NG - 1 - n, h_all).then_inc(y_neg, 1)
                if n:
                    subtract_neg(n - 1)
            subtract_neg(NG - 1)

            def inverse_std(t, b, made, veps_s, done):
                pool.wait_ge(made, t + 1)
                nc.gpsimd.tensor_tensor(veps[:, :], mv[:, b, 1:2], eps[:, :], ALU.add).then_inc(veps_s, 1)
                pool.wait_ge(veps_s, t + 1)
                nc.gpsimd.tensor_tensor(rstd[:, b:b + 1], veps[:, :], minus_half[:, :], ALU.pow).then_inc(done, 1)

            def add_h(t, b):
                pool.wait_ge(h1_made, t + 1)
                nc.gpsimd.tensor_tensor(hsum[:, :], hsum[:, :], xh[:, b, D:2 * D], ALU.add).then_inc(hsum_added, 1)

            pool.wait_ge(hsum_done, 1)
            nc.gpsimd.memset(hsum[:, :], 0.0)
            inverse_std(0, 0, stats_made, veps_made, rstd_made)
            with pool.Fori(0, (TILES - 2) // 2) as u:
                for k in range(2):
                    t = 2 * u + k + 1
                    inverse_std(t, 1 - k, stats_made, veps_made, rstd_made)
                    add_h(t - 1, k)
            inverse_std(TILES - 1, 1, stats_made, veps_made, rstd_made)
            add_h(TILES - 2, 0)
            add_h(TILES - 1, 1)
            pool.wait_ge(max1_in, 1)
            nc.gpsimd.partition_all_reduce(cst[:, 0:2], cst[:, 0:2], P, MAX).then_inc(max1_out, 1)
            pool.wait_ge(den_step, 7)

            def subtract1(n):
                g = pool_groups[n]
                pool.wait_ge(hi1, g + 1)
                denominator_columns(nc.gpsimd, wts_pos, 0, g)
                left_over(wts_pos, slots1[g], g).then_inc(left1, 1)

            for n, g in enumerate(pool_groups):
                pool.wait_ge(h1_in[g], 16)
                product(nc.gpsimd, slots1[g], 1, g, h1_all).then_inc(y1_pool, 1)
                if n == 1:
                    pool.wait_ge(den_step, 9)
                if n:
                    subtract1(n - 1)
            subtract1(len(pool_groups) - 1)
            with pool.Fori(0, JH) as u:
                for b in range(2):
                    inverse_std(2 * u + b, b, stats1, veps1, rstd1)

        @block.tensor
        def _(pe):
            def small_products():
                pe.wait_ge(const_in, 16 * CONSTS)
                pe.wait_ge(dve_const, 1)
                nc.tensor.matmul(small_ps[:, 0:2], w0_sb[:, :], a12_sb[:, :], start=True, stop=True)
                nc.tensor.matmul(small_ps[:, 2:4], rep[:, :], a12_sb[:, :], start=True, stop=True).then_inc(
                    small_done, 1)
                pe.wait_ge(h_rhs_ready, 2)

            def transpose_x(c, k, nth, older=True):
                pe.wait_ge(x_in_landed[k], nth)
                if older:
                    pe.wait_ge(xT_copied, c - 1)
                for i in range(XT):
                    last = nc.tensor.transpose(xT_ps[k % 2][:, i * P:(i + 1) * P], x_in[:, k, i, :], eye_sb[:, :])
                last.then_inc(xT_done, 1)

            def make_h(c, b, older=True):
                pe.wait_ge(xT_copied, c + 1)
                if older:
                    pe.wait_ge(h_out, c - 1)
                for i in range(XT):
                    last = nc.tensor.matmul(h_ps(b)[:, i // 2, i % 2, :], xT_sb[:, b, i * P:(i + 1) * P], h_rhs[:, :],
                                            start=True, stop=True)
                last.then_inc(h_done, 1)
                if older:
                    pe.wait_ge(s2_copied, c - 1)
                nc.tensor.matmul(s2_ps[b], rep[:, :], xT_sb[:, b, :], start=True, stop=True).then_inc(s2_done, 1)

            pe.wait_ge(eye_in, 16)
            for c in range(XSLOTS):
                transpose_x(c, c, 16, older=c >= 2)
                if c == 1:
                    small_products()
                if c:
                    make_h(c - 1, (c - 1) % 2, older=c >= 3)
            with pe.Fori(1, CHUNKS // XSLOTS) as u:
                for k in range(XSLOTS):
                    transpose_x(XSLOTS * u + k, k, 16 * u + 16)
                    make_h(XSLOTS * u + k - 1, (k + 1) % 2)
            make_h(CHUNKS - 1, 1)
            def pack(t, h, older=True):
                pe.wait_ge(pairs_made, 2 * t + h + 1)
                if older:
                    pe.wait_ge(words_made, 2 * t - 2 + h + 1)
                pe.sem_inc(pe_passed, 1)
                for j in range(JQ):
                    last = nc.tensor.matmul(pack_ps[h][:, WORDS * j:WORDS * (j + 1)],
                                            branch[:, 2 * h, P * j:P * (j + 1)].bitcast(F8),
                                            packer_sb[:, :], start=True, stop=True)
                last.then_inc(packed, 1)

            def multiply(t, b, jobs=()):
                pe.wait_ge(masks_made, t + 1)
                pe.wait_ge(acc_copied, t - 1)
                pe.sem_inc(pe_passed, 1)
                for j in range(TILES):
                    n, j = j, TILES - 1 - j
                    for kind, wts in ((1, wts_neg), (0, wts_pos)):
                        last = nc.tensor.matmul(acc_ps[b][kind][:, 0:COLS], masks[:, b, kind, j, :].bitcast(F8),
                                                wts[:, j, :], start=(n == 0), stop=(n == TILES - 1))
                    for at, job in jobs:
                        if n == at * TILES // 64:
                            job()
                last.then_inc(acc_done, 1)

            def transpose_x1(t, b):
                pe.wait_ge(x1_made, t + 1)
                nc.tensor.transpose(x1T_ps[:, 0:P], xh[:, b, 0:D], eye_sb[:, :]).then_inc(x1T_done, 1)

            def make_h1(t, older=True):
                pe.wait_ge(x1T_copied, t + 1)
                if older:
                    pe.wait_ge(h1_made, t)
                nc.tensor.matmul(h1_ps[:, 0:D], x1T_sb[:, :], w1_sb[:, :], start=True, stop=True).then_inc(h1_done, 1)

            def iteration(t, b, first=False, last=False):
                at, pack_at = (48, 60), [20, 38]
                if first:
                    at, pack_at = (58, 62), [22, 54]
                    jobs = [(44, lambda: transpose_x1(t - 2, b)), (50, lambda: make_h1(t - 2, older=False))]
                else:
                    jobs = []
                jobs += [(at[0], lambda: transpose_x1(t - 1, 1 - b)), (at[1], lambda: make_h1(t - 1))]
                if not last:
                    jobs += [(pack_at[h], lambda h=h: pack(t + 1, h)) for h in range(PAIRS)]
                multiply(t, b, jobs)

            pe.wait_ge(later_in, 16 * LATER)
            pe.wait_ge(h_out, CHUNKS)
            for h in range(PAIRS):
                pack(0, h, older=False)
            pe.wait_ge(s2_copied, CHUNKS)
            pe.wait_ge(xsum_ready, 1)
            nc.tensor.matmul(small_ps[:, 0:D], rep[:, :], h_rhs[:, 0:D], start=True, stop=True).then_inc(hsum_done, 1)

            def share(t, n):
                for j in range(TILES - 1 - GJ * n, TILES - 1 - GJ * (n + 1), -1):
                    for kind, wts in ((1, wts_neg), (0, wts_pos)):
                        last = nc.tensor.matmul(acc_ps[t][kind][:, 0:COLS], masks[:, t, kind, j, :].bitcast(F8),
                                                wts[:, j, :], start=(j == TILES - 1), stop=(j == 0))
                return last

            pe.wait_ge(masks_made, 1)
            for n in range(NG):
                for tile, q in pieces_of(n):
                    if q % 2:
                        pack(tile, q // 2)
                if n == early:
                    pe.wait_ge(masks_made, 2)
                    for m in range(early):
                        share(1, m)
                pe.wait_ge(lo_pos, n + 1)
                pe.wait_ge(lo_neg, n + 1)
                done = share(0, n)
                if n == NG - 1:
                    done.then_inc(acc_done, 1)
                if n >= early:
                    done = share(1, n)
            done.then_inc(acc_done, 1)
            iteration(2, 0, first=True)
            with pe.Fori(0, (TILES - 4) // 2) as u:
                for k in range(2):
                    iteration(2 * u + k + 3, 1 - k)
            iteration(TILES - 1, 1, last=True)
            transpose_x1(TILES - 1, 1)
            make_h1(TILES - 1)

            pe.wait_ge(hsum_added, TILES)
            pe.wait_ge(h1_made, TILES)
            nc.tensor.matmul(h1_ps[:, 0:D], ones[:, :], hsum[:, :], start=True, stop=True).then_inc(hsum_done, 1)

            pe.wait_ge(masks1_made, 2)
            for g in range(NG):
                if g in pool_groups:
                    pe.wait_ge(lo1_pool, pool_groups.index(g) + 1)
                else:
                    pe.wait_ge(lo1, dve_groups.index(g) + 1)
                for b in range(2):
                    for j in range(GJ * g, GJ * (g + 1)):
                        done = nc.tensor.matmul(acc_ps[b][0][:, 0:COLS], mask1(b, b)[:, j, :].bitcast(F8),
                                                wts_pos[:, j, :], start=(j == 0), stop=(j == TILES - 1))
                    if g == NG - 1:
                        done.then_inc(acc1_done, 1)

            def multiply1(t, b):
                pe.wait_ge(masks1_made, t + 1)
                pe.wait_ge(acc1_copied, t - 1)
                pe.sem_inc(pe_passed, 1)
                for j in range(TILES):
                    last = nc.tensor.matmul(acc_ps[b][0][:, 0:COLS], mask1(t, b)[:, j, :].bitcast(F8),
                                            wts_pos[:, j, :], start=(j == 0), stop=(j == TILES - 1))
                last.then_inc(acc1_done, 1)

            multiply1(2, 0)
            multiply1(3, 1)
            with pe.Fori(2, JH) as u:
                for b in range(2):
                    multiply1(2 * u + b, b)


def kernel(x, adj, L0_gnn_W, L0_gnn_b_W, L0_gnn_a_vec, L0_gnn_b_a, L1_gnn_W_fc, L1_gnn_b_fc, L1_gnn_w_att,
           L1_gnn_b_att):
    import ml_dtypes
    import numpy as np
    import concourse.bacc as bacc
    from concourse import mybir
    from concourse.bass_utils import run_bass_kernel_spmd

    i = np.arange(128)
    place = 2.0 ** 9 * 16.0 ** (i // 64) * 256.0 ** (i % 2)
    packer = np.where((i % 64 // 2)[:, None] == np.arange(32)[None, :], place[:, None], 0.0).astype(ml_dtypes.bfloat16)
    arrays = {
        "x": x, "adj": adj, "w0": L0_gnn_W, "w0t": np.asarray(L0_gnn_W).T, "b0_col": np.reshape(L0_gnn_b_W, (-1, 1)),
        "b0": np.reshape(L0_gnn_b_W, (1, -1)),
        "a12": np.reshape(L0_gnn_a_vec, (2, -1)).T, "ba": np.reshape(L0_gnn_b_a, (1, 1)),
        "w1": L1_gnn_W_fc, "b1": np.reshape(L1_gnn_b_fc, (1, -1)), "watt": np.reshape(L1_gnn_w_att, (1, -1)),
        "packer": packer, "eye": np.eye(128, dtype=np.float32),
    }
    arrays = {f"in_{name}": np.ascontiguousarray(a) for name, a in arrays.items()}
    nc = bacc.Bacc("TRN2", target_bir_lowering=False, num_devices=1)
    ins = [nc.dram_tensor(name, a.shape, mybir.dt.from_np(a.dtype), kind="ExternalInput").ap()
           for name, a in arrays.items()]
    out = nc.dram_tensor("out", x.shape, mybir.dt.float32, kind="ExternalOutput").ap()
    build_two_layer_gat(nc, *ins, out)
    return run_bass_kernel_spmd(nc, [arrays], core_ids=[0]).results[0]["out"]
```
